# Optimizing a Trainium2 kernel written in Bass

```python
import numpy as np
import jax
import jax.numpy as jnp

def _softmax(x, axis=-1):
    return jax.nn.softmax(x, axis=axis)

def _gelu(x):
    return jax.nn.gelu(x, approximate=True)

def _silu(x):
    return jax.nn.silu(x)

def _sigmoid(x):
    return jax.nn.sigmoid(x)

def _layernorm(x, axis=-1, eps=1e-05):
    m = jnp.mean(x, axis=axis, keepdims=True)
    v = jnp.var(x, axis=axis, keepdims=True)
    return (x - m) / jnp.sqrt(v + eps)

def _scatter_add(tgt, idx, src, axis=0):
    return tgt.at[idx].add(src)

def _segment_sum(src, seg, n):
    return jax.ops.segment_sum(src, seg, n)
kernel_name = 'mk_hybrid_d1_jaxref_r8_e32cde'

def setup_inputs(seed: int=0):
    np.random.seed(seed)
    _w = jnp.asarray

    def _L0_attn_a_setup():
        import jax, jax.numpy as jnp
        import numpy as np
        HIDDEN = 128
        N_HEADS = 16
        D_HEAD = HIDDEN // N_HEADS

        def _rope(q, k):
            B, H, N, d = q.shape
            inv_freq = 1.0 / 10000.0 ** (jnp.arange(0, d, 2, dtype=jnp.float32) / d)
            pos = jnp.arange(N, dtype=jnp.float32)
            thetas = pos[:, None] * inv_freq[None, :]
            cos, sin = (jnp.cos(thetas), jnp.sin(thetas))

            def rot(x):
                xp = x.reshape(B, H, N, d // 2, 2)
                xx, xy = (xp[..., 0], xp[..., 1])
                rx = xx * cos - xy * sin
                ry = xx * sin + xy * cos
                return jnp.stack([rx, ry], axis=-1).reshape(B, H, N, d)
            return (rot(q), rot(k))
        key = jax.random.key(seed)
        ks = jax.random.split(key, 9)
        B, N, Hd = (4, 256, HIDDEN)
        s = 1.0 / np.sqrt(Hd)
        return {'x': jax.random.normal(ks[0], (B, N, Hd), jnp.float32), 'Wq': jax.random.normal(ks[1], (Hd, Hd), jnp.float32) * s, 'bq': jax.random.normal(ks[2], (Hd,), jnp.float32) * 0.02, 'Wk': jax.random.normal(ks[3], (Hd, Hd), jnp.float32) * s, 'bk': jax.random.normal(ks[4], (Hd,), jnp.float32) * 0.02, 'Wv': jax.random.normal(ks[5], (Hd, Hd), jnp.float32) * s, 'bv': jax.random.normal(ks[6], (Hd,), jnp.float32) * 0.02, 'Wo': jax.random.normal(ks[7], (Hd, Hd), jnp.float32) * s, 'bo': jax.random.normal(ks[8], (Hd,), jnp.float32) * 0.02}
    _L0_attn_a_in = _L0_attn_a_setup()

    def _L0_attn_b_setup():
        import jax, jax.numpy as jnp
        import numpy as np
        import math
        N_EMBD = 128
        N_HEAD = 16
        HEAD = N_EMBD // N_HEAD
        LAYER_IDX = 2
        LAMBDA_INIT = 0.8 - 0.6 * math.exp(-0.3 * (LAYER_IDX - 1))
        BN_EPS = 1e-05
        RMS_EPS = 1e-05

        def _heads(y, B, T, d):
            return y.reshape(B, T, N_HEAD, d).transpose(0, 2, 1, 3)
        key = jax.random.key(seed)
        ks = jax.random.split(key, 16)
        B, T = (4, 128)
        s = 1.0 / math.sqrt(N_EMBD)
        return {'x': jax.random.normal(ks[0], (B, T, N_EMBD), jnp.float32), 'q1_w': jax.random.normal(ks[1], (N_EMBD, N_EMBD), jnp.float32) * s, 'q2_w': jax.random.normal(ks[2], (N_EMBD, N_EMBD), jnp.float32) * s, 'k1_w': jax.random.normal(ks[3], (N_EMBD, N_EMBD), jnp.float32) * s, 'k2_w': jax.random.normal(ks[4], (N_EMBD, N_EMBD), jnp.float32) * s, 'v_w': jax.random.normal(ks[5], (2 * N_EMBD, N_EMBD), jnp.float32) * s, 'c_w': jax.random.normal(ks[6], (N_EMBD, 2 * N_EMBD), jnp.float32) * s, 'subln_w': jnp.ones((2 * HEAD,), jnp.float32), 'lq1': jax.random.normal(ks[7], (HEAD,), jnp.float32) * 0.1, 'lk1': jax.random.normal(ks[8], (HEAD,), jnp.float32) * 0.1, 'lq2': jax.random.normal(ks[9], (HEAD,), jnp.float32) * 0.1, 'lk2': jax.random.normal(ks[10], (HEAD,), jnp.float32) * 0.1, 'bn_gamma': jnp.ones((N_EMBD,), jnp.float32), 'bn_beta': jnp.zeros((N_EMBD,), jnp.float32)}
    _L0_attn_b_in = _L0_attn_b_setup()

    def _L0_ffn_setup():
        import jax, jax.numpy as jnp
        import numpy as np
        NUM_EXPERTS = 8
        N_EMBD = 128
        D_FF = 4 * N_EMBD
        B, S = (4, 256)
        key = jax.random.key(seed)
        ks = jax.random.split(key, 6)
        x = jax.random.normal(ks[0], (B, S, N_EMBD), dtype=jnp.float32)
        gate_w = jax.random.normal(ks[1], (N_EMBD, NUM_EXPERTS), dtype=jnp.float32) * 0.02
        w1 = jax.random.normal(ks[2], (NUM_EXPERTS, N_EMBD, D_FF), dtype=jnp.float32) * 0.02
        b1 = jnp.zeros((NUM_EXPERTS, D_FF), dtype=jnp.float32)
        w2 = jax.random.normal(ks[3], (NUM_EXPERTS, D_FF, N_EMBD), dtype=jnp.float32) * 0.02
        b2 = jnp.zeros((NUM_EXPERTS, N_EMBD), dtype=jnp.float32)
        return {'x': x, 'gate_w': gate_w, 'w1': w1, 'b1': b1, 'w2': w2, 'b2': b2}
    _L0_ffn_in = _L0_ffn_setup()
    _d = {'L0_attn_a_x': _L0_attn_a_in['x'], 'L0_attn_a_Wq': _L0_attn_a_in['Wq'], 'L0_attn_a_bq': _L0_attn_a_in['bq'], 'L0_attn_a_Wk': _L0_attn_a_in['Wk'], 'L0_attn_a_bk': _L0_attn_a_in['bk'], 'L0_attn_a_Wv': _L0_attn_a_in['Wv'], 'L0_attn_a_bv': _L0_attn_a_in['bv'], 'L0_attn_a_Wo': _L0_attn_a_in['Wo'], 'L0_attn_a_bo': _L0_attn_a_in['bo'], 'L0_attn_b_q1_w': _L0_attn_b_in['q1_w'], 'L0_attn_b_q2_w': _L0_attn_b_in['q2_w'], 'L0_attn_b_k1_w': _L0_attn_b_in['k1_w'], 'L0_attn_b_k2_w': _L0_attn_b_in['k2_w'], 'L0_attn_b_v_w': _L0_attn_b_in['v_w'], 'L0_attn_b_c_w': _L0_attn_b_in['c_w'], 'L0_attn_b_subln_w': _L0_attn_b_in['subln_w'], 'L0_attn_b_lq1': _L0_attn_b_in['lq1'], 'L0_attn_b_lk1': _L0_attn_b_in['lk1'], 'L0_attn_b_lq2': _L0_attn_b_in['lq2'], 'L0_attn_b_lk2': _L0_attn_b_in['lk2'], 'L0_attn_b_bn_gamma': _L0_attn_b_in['bn_gamma'], 'L0_attn_b_bn_beta': _L0_attn_b_in['bn_beta'], 'L0_ffn_gate_w': _L0_ffn_in['gate_w'], 'L0_ffn_w1': _L0_ffn_in['w1'], 'L0_ffn_b1': _L0_ffn_in['b1'], 'L0_ffn_w2': _L0_ffn_in['w2'], 'L0_ffn_b2': _L0_ffn_in['b2']}
    _x0 = _d['L0_attn_a_x']
    _d['L0_attn_a_x'] = jax.random.normal(jax.random.fold_in(jax.random.key(seed), 1), (2, 1024, 128), dtype=_x0.dtype)
    del _x0
    return _d

def reference(L0_attn_a_x, L0_attn_a_Wq, L0_attn_a_bq, L0_attn_a_Wk, L0_attn_a_bk, L0_attn_a_Wv, L0_attn_a_bv, L0_attn_a_Wo, L0_attn_a_bo, L0_attn_b_q1_w, L0_attn_b_q2_w, L0_attn_b_k1_w, L0_attn_b_k2_w, L0_attn_b_v_w, L0_attn_b_c_w, L0_attn_b_subln_w, L0_attn_b_lq1, L0_attn_b_lk1, L0_attn_b_lq2, L0_attn_b_lk2, L0_attn_b_bn_gamma, L0_attn_b_bn_beta, L0_ffn_gate_w, L0_ffn_w1, L0_ffn_b1, L0_ffn_w2, L0_ffn_b2):

    def _L0_attn_a_ref(x, Wq, bq, Wk, bk, Wv, bv, Wo, bo):
        import jax, jax.numpy as jnp
        import numpy as np
        HIDDEN = 128
        N_HEADS = 16
        D_HEAD = HIDDEN // N_HEADS

        def _rope(q, k):
            B, H, N, d = q.shape
            inv_freq = 1.0 / 10000.0 ** (jnp.arange(0, d, 2, dtype=jnp.float32) / d)
            pos = jnp.arange(N, dtype=jnp.float32)
            thetas = pos[:, None] * inv_freq[None, :]
            cos, sin = (jnp.cos(thetas), jnp.sin(thetas))

            def rot(x):
                xp = x.reshape(B, H, N, d // 2, 2)
                xx, xy = (xp[..., 0], xp[..., 1])
                rx = xx * cos - xy * sin
                ry = xx * sin + xy * cos
                return jnp.stack([rx, ry], axis=-1).reshape(B, H, N, d)
            return (rot(q), rot(k))
        B, N, _ = x.shape
        H, d = (N_HEADS, D_HEAD)
        q = (x @ Wq.T + bq).reshape(B, N, H, d).transpose(0, 2, 1, 3)
        k = (x @ Wk.T + bk).reshape(B, N, H, d).transpose(0, 2, 1, 3)
        v = (x @ Wv.T + bv).reshape(B, N, H, d).transpose(0, 2, 1, 3)
        q, k = _rope(q, k)
        scores = jnp.einsum('bhnd,bhmd->bhnm', q, k) / jnp.sqrt(jnp.asarray(d, x.dtype))
        attn = jax.nn.softmax(scores, axis=-1)
        out = jnp.einsum('bhnm,bhmd->bhnd', attn, v)
        out = out.transpose(0, 2, 1, 3).reshape(B, N, H * d)
        return out @ Wo.T + bo

    def _L0_attn_b_ref(x, q1_w, q2_w, k1_w, k2_w, v_w, c_w, subln_w, lq1, lk1, lq2, lk2, bn_gamma, bn_beta):
        import jax, jax.numpy as jnp
        import numpy as np
        import math
        N_EMBD = 128
        N_HEAD = 16
        HEAD = N_EMBD // N_HEAD
        LAYER_IDX = 2
        LAMBDA_INIT = 0.8 - 0.6 * math.exp(-0.3 * (LAYER_IDX - 1))
        BN_EPS = 1e-05
        RMS_EPS = 1e-05

        def _heads(y, B, T, d):
            return y.reshape(B, T, N_HEAD, d).transpose(0, 2, 1, 3)
        B, T, C = x.shape
        mean = jnp.mean(x, axis=(0, 1))
        var = jnp.var(x, axis=(0, 1))
        xn = (x - mean) * jax.lax.rsqrt(var + BN_EPS) * bn_gamma + bn_beta
        q1 = _heads(xn @ q1_w.T, B, T, HEAD)
        q2 = _heads(xn @ q2_w.T, B, T, HEAD)
        k1 = _heads(xn @ k1_w.T, B, T, HEAD)
        k2 = _heads(xn @ k2_w.T, B, T, HEAD)
        v = _heads(xn @ v_w.T, B, T, 2 * HEAD)
        scale = 1.0 / math.sqrt(HEAD)
        att1 = jax.nn.softmax(jnp.einsum('bhtd,bhsd->bhts', q1, k1) * scale, axis=-1)
        att2 = jax.nn.softmax(jnp.einsum('bhtd,bhsd->bhts', q2, k2) * scale, axis=-1)
        lam = jnp.exp(jnp.sum(lq1 * lk1)) - jnp.exp(jnp.sum(lq2 * lk2)) + LAMBDA_INIT
        att = att1 - lam * att2
        y = jnp.einsum('bhts,bhse->bhte', att, v)
        y = y * jax.lax.rsqrt(jnp.mean(y * y, axis=-1, keepdims=True) + RMS_EPS) * subln_w
        y = y * (1.0 - LAMBDA_INIT)
        y = y.transpose(0, 2, 1, 3).reshape(B, T, 2 * C)
        return y @ c_w.T

    def _L0_ffn_ref(x, gate_w, w1, b1, w2, b2):
        import jax, jax.numpy as jnp
        import numpy as np
        NUM_EXPERTS = 8
        N_EMBD = 128
        D_FF = 4 * N_EMBD
        B, S = (4, 256)
        Bb, Ss, D = x.shape
        x_flat = x.reshape(-1, D)
        router_logits = x_flat @ gate_w
        router_probs = jax.nn.softmax(router_logits, axis=-1)
        expert_idx = jnp.argmax(router_probs, axis=-1)
        expert_w = jnp.take_along_axis(router_probs, expert_idx[:, None], axis=1)[:, 0]
        out = jnp.zeros_like(x_flat)
        for e in range(NUM_EXPERTS):
            h = jax.nn.gelu(x_flat @ w1[e] + b1[e], approximate=False)
            y = h @ w2[e] + b2[e]
            sel = expert_idx == e
            out = out + jnp.where(sel, expert_w, 0.0)[:, None] * y
        return out.reshape(Bb, Ss, D)
    x = L0_attn_a_x
    x = x + _L0_attn_a_ref(_layernorm(x, axis=-1), L0_attn_a_Wq, L0_attn_a_bq, L0_attn_a_Wk, L0_attn_a_bk, L0_attn_a_Wv, L0_attn_a_bv, L0_attn_a_Wo, L0_attn_a_bo)
    x = x + _L0_ffn_ref(_layernorm(x, axis=-1), L0_ffn_gate_w, L0_ffn_w1, L0_ffn_b1, L0_ffn_w2, L0_ffn_b2)
    x = x + _L0_attn_b_ref(_layernorm(x, axis=-1), L0_attn_b_q1_w, L0_attn_b_q2_w, L0_attn_b_k1_w, L0_attn_b_k2_w, L0_attn_b_v_w, L0_attn_b_c_w, L0_attn_b_subln_w, L0_attn_b_lq1, L0_attn_b_lk1, L0_attn_b_lq2, L0_attn_b_lk2, L0_attn_b_bn_gamma, L0_attn_b_bn_beta)
    x = x + _L0_ffn_ref(_layernorm(x, axis=-1), L0_ffn_gate_w, L0_ffn_w1, L0_ffn_b1, L0_ffn_w2, L0_ffn_b2)
    return x

_drawn_inputs = setup_inputs


def setup_inputs(seed=0):
    import zlib

    import numpy as np

    out = dict(_drawn_inputs(seed))
    spreads = {'L0_attn_b_subln_w': (1.0, 0.2),
     'L0_attn_b_bn_gamma': (1.0, 0.2),
     'L0_attn_b_bn_beta': (0.0, 0.1),
     'L0_ffn_b1': (0.0, 0.8),
     'L0_ffn_b2': (0.0, 0.313)}
    factors = {'L0_attn_a_bq': 8.0,
     'L0_attn_a_bk': 8.0,
     'L0_attn_a_bv': 3.441,
     'L0_attn_a_bo': 3.613,
     'L0_attn_b_lq2': 4.009,
     'L0_attn_b_lk2': 8.0,
     'L0_ffn_w1': 4.242,
     'L0_ffn_w2': 3.824}
    for name, (base, spread) in spreads.items():
        noise = np.random.default_rng([zlib.crc32(name.encode()), seed]).standard_normal(out[name].shape)
        drawn = base * np.exp(spread * noise) if base else spread * noise
        out[name] = jnp.asarray(drawn.astype(out[name].dtype))
    for name, factor in factors.items():
        out[name] = (out[name] * factor).astype(out[name].dtype)
    return out
```

```python
import math
from contextlib import ExitStack

import numpy as np
import concourse.bass as bass
from concourse import mybir

F32 = mybir.dt.float32
BF16 = mybir.dt.bfloat16
ACT = mybir.ActivationFunctionType
ALU = mybir.AluOpType
AX = mybir.AxisListType.X

P = 128
B, N, D = 2, 1024, 128
TOK = B * N
TPB = N // P
TILES = TOK // P
CH = 512
CHUNKS = TOK // CH
TPC = CH // P
H, DH = 16, 8
HG = 4
GPB = H // HG
GROUPS = B * GPB
VC = 32
E, FF = 8, 512
FC = FF // P
LN_EPS = 1e-5
LAMBDA_INIT = 0.8 - 0.6 * math.exp(-0.3)
SCALE = 1.0 / math.sqrt(DH)

PRODUCTS = [(0, 0), (0, 1), (1, 0), (1, 1), (0, 2), (2, 0)]
HALF = 64
MAXROW = DH * len(PRODUCTS)


def is_first(g):
    return isinstance(g, int) and g == 0


def is_last(g):
    return isinstance(g, int) and g == GROUPS - 1


class Kit:

    def __init__(self, nc, life):
        self.nc, self.life, self.sems = nc, life, []

    def sb(self, name, shape, dtype=F32):
        return self.life.enter_context(self.nc.sbuf_tensor(name, shape, dtype))

    def sem(self, name):
        self.sems.append(self.nc.alloc_semaphore(name))
        return self.sems[-1]

    def release(self):
        self.nc.clear_and_free_semaphores(self.sems)
        self.nc.all_engine_barrier()


def layernorm_transposed(nc, kit, tag, x, xT, bank, ident, extra_loads=None):
    with ExitStack() as life:
        k = Kit(nc, life)
        stats = k.sb(f"stats_{tag}", [P, TILES, 6])
        mv = k.sb(f"mv_{tag}", [P, TILES, 2])
        std = k.sb(f"std_{tag}", [P, TILES])
        rstd = k.sb(f"rstd_{tag}", [P, TILES])
        xn = k.sb(f"xn_{tag}", [P, TILES, D])
        stats_done, mv_done = k.sem(f"stats_done_{tag}"), k.sem(f"mv_done_{tag}")
        std_done, rstd_done = k.sem(f"std_done_{tag}"), k.sem(f"rstd_done_{tag}")
        xn_done, turned = k.sem(f"xn_done_{tag}"), k.sem(f"turned_{tag}")
        copied = k.sem(f"copied_{tag}")
        with nc.Block() as block:

            @block.vector
            def _(dve):
                for t in range(TILES):
                    dve.bn_stats(stats[:, t, :], x[:, t, :]).then_inc(stats_done, 1)
                dve.wait_ge(stats_done, TILES)
                for t in range(TILES):
                    dve.bn_aggr(mv[:, t, :], stats[:, t, :]).then_inc(mv_done, 1)
                dve.wait_ge(std_done, 1)
                dve.reciprocal(rstd[:, :], std[:, :]).then_inc(rstd_done, 1)
                dve.wait_ge(rstd_done, 1)
                for t in range(TILES):
                    dve.tensor_scalar(xn[:, t, :], x[:, t, :], mv[:, t, 0:1], rstd[:, t:t + 1],
                                      ALU.subtract, ALU.mult).then_inc(xn_done, 1)

            @block.scalar
            def _(act):
                act.wait_ge(mv_done, TILES)
                act.activation(std[:, :], mv[:, :, 1], ACT.Sqrt, bias=LN_EPS).then_inc(std_done, 1)
                for c in range(CHUNKS):
                    act.wait_ge(turned, c + 1)
                    act.copy(xT[:, c * CH:(c + 1) * CH], bank[c % 2][:, :]).then_inc(copied, 1)
                act.wait_ge(copied, CHUNKS)

            @block.tensor
            def _(pe):
                for c in range(CHUNKS):
                    pe.wait_ge(xn_done, TPC * (c + 1))
                    if c >= 2:
                        pe.wait_ge(copied, c - 1)
                    for i in range(TPC):
                        last = pe.transpose(bank[c % 2][:, i * P:(i + 1) * P], xn[:, c * TPC + i, :], ident)
                    last.then_inc(turned, 1)

        k.release()


def attention(nc, kit, tag, qs, ks, vt, o, bank, ident, identb, e_dim, finish):
    STEPS = 2 * TPB
    LEAD = 4
    with ExitStack() as life:
        k = Kit(nc, life)
        vs = k.sb(f"vs_{tag}", [P, TPB, HG, VC])
        probs = k.sb(f"probs_{tag}", [P, 2, 2, 2, CH])
        ots = k.sb(f"ots_{tag}", [P, CH])
        mx = k.sb(f"mx_{tag}", [P, HG, TPB, 2])
        nmax = k.sb(f"nmax_{tag}", [P, TPB, HG])
        nmaxb = k.sb(f"nmaxb_{tag}", [P, TPB, HG, 2], BF16)
        maxrows = k.sb(f"maxrows_{tag}", [HG * 2, N], BF16)
        rec = k.sb(f"rec_{tag}", [P, TPC, HG])
        tmp = k.sb(f"tmp_{tag}", [P, TPC, HG, e_dim])
        names = ["max_scored", "max_taken", "max_joined", "max_split", "max_turned", "max_copied",
                 "max_rows", "scored", "exped", "multiplied", "v_ones", "v_staged", "o_copied",
                 "o_turned", "turn_read", "o_rec", "o_done"]
        s = {n: k.sem(f"{n}_{tag}") for n in names}
        score_bank = [[bank[0], bank[1]], [bank[2], bank[3]]]
        max_bank = [bank[4], bank[5]]
        out_bank, turn_bank = bank[6], bank[7]
        turnb = turn_bank[:, :].bitcast(BF16)

        def q_at(g, h, first, n):
            return qs[:, bass.ds((g * HG + h) * N + first, n)]

        def k_at(g, h, first, n):
            return ks[:, bass.ds((g * (HG // 2) + h // 2) * N + first, n)]

        with nc.Block() as block:

            @block.tensor
            def _(pe):
                def max_score(g, step, h):
                    tile = (g * STEPS + step) * HG + h
                    if not (is_first(g) and step == 0 and h < 2):
                        pe.wait_ge(s["max_taken"], tile - 1)
                    pe.matmul(max_bank[h % 2][:, :], q_at(g, h, (step // 2) * P, P),
                              k_at(g, h, (step % 2) * CH, CH), start=True, stop=True
                              ).then_inc(s["max_scored"], 1)

                def turn_max(g):
                    pe.wait_ge(s["max_split"], 2 * (g + 1))
                    if not is_first(g):
                        pe.wait_ge(s["turn_read"], 2 * g - 1)
                    for j in range(TPB):
                        last = pe.transpose(turnb[0:HG * 2, j * P:(j + 1) * P],
                                            nmaxb[:, j, :, :].rearrange("p h c -> p (h c)"), identb)
                    last.then_inc(s["max_turned"], 1)

                def scores(g, step, pair):
                    u = (g * STEPS + step) * 2 + pair
                    if step == 0 and pair == 0:
                        pe.wait_ge(s["max_rows"], 16 * HG * (g + 1))
                    if not (is_first(g) and step == 0):
                        pe.wait_ge(s["exped"], u - 1)
                    for i in range(2):
                        h = 2 * pair + i
                        last = pe.matmul(score_bank[pair][i][:, :], k_at(g, h, (step % TPB) * P, P),
                                         q_at(g, h, (step // TPB) * CH, CH), start=True, stop=True)
                    last.then_inc(s["scored"], 1)

                def multiply(g, step):
                    j = step % TPB
                    kk = g * STEPS + step
                    pe.wait_ge(s["exped"], 2 * (kk + 1))
                    if step == 0:
                        pe.wait_ge(s["v_staged"], 2 * g + 1)
                    if step == TPB - 1:
                        pe.wait_ge(s["v_staged"], 2 * g + 2)
                    if j == 0 and not (is_first(g) and step == 0):
                        pe.wait_ge(s["o_copied"], 2 * g + step // TPB)
                    for h in range(HG):
                        last = pe.matmul(out_bank[VC * h:VC * (h + 1), :], vs[:, j, h, :],
                                         probs[:, step % 2, h // 2, h % 2, :],
                                         start=(j == 0), stop=(j == TPB - 1))
                    last.then_inc(s["multiplied"], 1)

                def turn_out(g, half):
                    q = 2 * g + half
                    pe.wait_ge(s["o_copied"], q + 1)
                    if half == 0 and not is_first(g):
                        pe.wait_ge(s["turn_read"], q)
                    elif is_last(g):
                        pe.wait_ge(s["turn_read"], q)
                    elif half == 1:
                        pe.wait_ge(s["max_copied"], g + 2)
                    else:
                        pe.wait_ge(s["max_copied"], 1)
                    for i in range(TPC):
                        last = pe.transpose(turn_bank[:, i * P:(i + 1) * P], ots[:, i * P:(i + 1) * P], ident)
                    last.then_inc(s["o_turned"], 1)

                def group(g, first=False, last=False, next_last=False):
                    for step in range(STEPS):
                        ahead = step + LEAD
                        for pair in range(2):
                            scores(g, step, pair)
                            for h in range(2 * pair, 2 * pair + 2):
                                if ahead < STEPS and not last:
                                    max_score(g + 1, ahead, h)
                                elif ahead >= STEPS and not last and not next_last:
                                    max_score(g + 2, ahead - STEPS, h)
                        if step > 0:
                            multiply(g, step - 1)
                        elif not first:
                            multiply(g - 1, STEPS - 1)
                        if step == 1 and not first:
                            turn_out(g - 1, 1)
                        if step == TPB + 1:
                            turn_out(g, 0)
                        if step == STEPS - LEAD and not last:
                            turn_max(g + 1)

                for step in range(STEPS):
                    for h in range(HG):
                        max_score(0, step, h)
                turn_max(0)
                for step in range(LEAD):
                    for h in range(HG):
                        max_score(1, step, h)
                group(0, first=True)
                with pe.Fori(1, GROUPS - 2) as g:
                    group(g)
                group(GROUPS - 2, next_last=True)
                group(GROUPS - 1, last=True)
                multiply(GROUPS - 1, STEPS - 1)
                turn_out(GROUPS - 1, 1)

            @block.scalar
            def _(act):
                def exponentials(g, step):
                    kk = g * STEPS + step
                    for pair in range(2):
                        act.wait_ge(s["scored"], 2 * kk + pair + 1)
                        if not (is_first(g) and step < 2):
                            act.wait_ge(s["multiplied"], kk - 1)
                        for i in range(2):
                            last = act.activation(probs[:, step % 2, pair, i, :], score_bank[pair][i][:, :],
                                                  ACT.Exp, scale=SCALE)
                        last.then_inc(s["exped"], 1)

                def copy_out(g, half):
                    q = 2 * g + half
                    act.wait_ge(s["multiplied"], TPB * (q + 1))
                    if not (is_first(g) and half == 0):
                        act.wait_ge(s["o_turned"], q)
                    act.copy(ots[:, :], out_bank[:, :]).then_inc(s["o_copied"], 1)

                def copy_max(g):
                    act.wait_ge(s["max_turned"], g + 1)
                    if not is_first(g):
                        act.wait_ge(s["max_rows"], 16 * HG * g)
                    act.copy(maxrows[:, :], turnb[0:HG * 2, :]).then_inc(s["max_copied"], 1)

                def group(g, first=False, last=False):
                    for step in range(STEPS):
                        exponentials(g, step)
                        if step == 0 and not first:
                            copy_out(g - 1, 1)
                        if step == TPB:
                            copy_out(g, 0)
                        if step == STEPS - LEAD + 1 and not last:
                            copy_max(g + 1)

                copy_max(0)
                group(0, first=True)
                with act.Fori(1, GROUPS - 1) as g:
                    group(g)
                group(GROUPS - 1, last=True)
                copy_out(GROUPS - 1, 1)

            @block.vector
            def _(dve):
                def take_max(g, step):
                    for h in range(HG):
                        dve.wait_ge(s["max_scored"], (g * STEPS + step) * HG + h + 1)
                        dve.tensor_reduce(mx[:, h, step // 2, step % 2:step % 2 + 1], max_bank[h % 2][:, :],
                                          AX, ALU.max).then_inc(s["max_taken"], 1)

                def split_max(g):
                    dve.wait_ge(s["max_taken"], HG * STEPS * (g + 1))
                    if not is_first(g):
                        dve.wait_ge(s["max_turned"], g)
                    dve.tensor_tensor(nmax[:, :, :].rearrange("p j h -> p h j"), mx[:, :, :, 0], mx[:, :, :, 1],
                                      ALU.max).then_inc(s["max_joined"], 1)
                    dve.wait_ge(s["max_joined"], g + 1)
                    dve.tensor_scalar(nmaxb[:, :, :, 0], nmax[:, :, :], -1.0, None, ALU.mult
                                      ).then_inc(s["max_split"], 1)
                    dve.wait_ge(s["max_split"], 2 * g + 1)
                    dve.scalar_tensor_tensor(out=nmaxb[:, :, :, 1], in0=nmax[:, :, :], scalar=-1.0,
                                             in1=nmaxb[:, :, :, 0], op0=ALU.mult, op1=ALU.subtract
                                             ).then_inc(s["max_split"], 1)

                def where(g, half):
                    tiles = o[:, :].rearrange("p (t w) -> p t w", t=TILES)
                    return tiles[:, bass.ds((g // GPB) * TPB + half * TPC, TPC),
                                 bass.ds((g % GPB) * HG * e_dim, HG * e_dim)]

                def divide(g, half):
                    q = 2 * g + half
                    dve.wait_ge(s["o_turned"], q + 1)
                    t = turn_bank[:, :].rearrange("p (i h c) -> p i h c", i=TPC, h=HG)
                    dve.reciprocal(rec[:, :, :], t[:, :, :, e_dim]).then_inc(s["o_rec"], 1)
                    dve.wait_ge(s["o_rec"], q + 1)
                    finish(dve, t[:, :, :, 0:e_dim],
                           rec[:, :, :].unsqueeze(3).to_broadcast([P, TPC, HG, e_dim]),
                           where(g, half), tmp, q, s)

                def group(g, first=False, last=False, next_last=False):
                    for step in range(STEPS):
                        ahead = step + LEAD
                        if ahead < STEPS:
                            if not last:
                                take_max(g + 1, ahead)
                        elif not last and not next_last:
                            take_max(g + 2, ahead - STEPS)
                        if ahead == STEPS - 1 and not last:
                            split_max(g + 1)
                        if step == 1 and not first:
                            divide(g - 1, 1)
                        if step == TPB + 1:
                            divide(g, 0)

                for step in range(STEPS):
                    take_max(0, step)
                split_max(0)
                for step in range(LEAD):
                    take_max(1, step)
                group(0, first=True)
                with dve.Fori(1, GROUPS - 2) as g:
                    group(g)
                group(GROUPS - 2, next_last=True)
                group(GROUPS - 1, last=True)
                divide(GROUPS - 1, 1)

            @block.gpsimd
            def _(pool):
                pool.memset(vs[:, :, :, :], 1.0).then_inc(s["v_ones"], 1)
                pool.wait_ge(s["v_ones"], 1)

                def stage(g):
                    v = vt[:, bass.ds(g * TPB * HG * e_dim, TPB * HG * e_dim)].rearrange(
                        "p (j h e) -> p j h e", j=TPB, h=HG)
                    if not is_first(g):
                        pool.wait_ge(s["multiplied"], g * STEPS - 1)
                    pool.tensor_copy(vs[:, 0:TPB - 1, :, 0:e_dim], v[:, 0:TPB - 1]).then_inc(s["v_staged"], 1)
                    if not is_first(g):
                        pool.wait_ge(s["multiplied"], g * STEPS)
                    pool.tensor_copy(vs[:, TPB - 1, :, 0:e_dim], v[:, TPB - 1]).then_inc(s["v_staged"], 1)

                stage(0)
                with pool.Fori(1, GROUPS) as g:
                    stage(g)

            @block.sync
            def _(sync):
                def write_max(g):
                    sync.wait_ge(s["max_copied"], g + 1)
                    for h in range(HG):
                        row = HALF * (h % 2) + MAXROW
                        sync.dma_start(qs[row:row + 2, bass.ds((g * HG + h) * N, N)],
                                       maxrows[2 * h:2 * h + 2, :]).then_inc(s["max_rows"], 16)

                write_max(0)
                with sync.Fori(1, GROUPS) as g:
                    write_max(g)
                sync.wait_ge(s["max_rows"], 16 * HG * GROUPS)

        k.release()


def prepare(nc, kit, tag, xT, q_weights, k_weights, v, parts_dram, qs, ks, bank, rope=None, rezero=False):
    UNITS = 2 * CHUNKS
    with ExitStack() as life:
        k = Kit(nc, life)
        parts = k.sb(f"parts_{tag}", [P, 2, 3, CH], BF16)
        rest = k.sb(f"rest_{tag}", [P, 2, CH])
        x32 = k.sb(f"x32_{tag}", [P, 2, CH]) if rope else None
        t1 = k.sb(f"t1_{tag}", [P, 2, CH]) if rope else None
        t2 = k.sb(f"t2_{tag}", [P, 2, CH]) if rope else None
        names = ["projected", "rot1", "rot2", "rotated", "high", "minus_high", "mid", "low", "parts_out0", "parts_out1",
                 "stacked", "zeroed", "v_done", "v_taken"]
        s = {n: k.sem(f"{n}_{tag}") for n in names}
        per = 2 if rope else 1
        unit = lambda u: (u % 2, u // 2)
        weights = lambda side: (q_weights, k_weights)[side]
        v_w, vt, v_bias, e_dim = v
        width = H * e_dim
        tiles_per_bank = CH // width
        V_UNITS = TILES // tiles_per_bank

        with nc.Block() as block:

            @block.tensor
            def _(pe):
                for u in range(UNITS):
                    side, c = unit(u)
                    if u >= 2:
                        pe.wait_ge(s["rot2"] if rope else s["minus_high"], u - 1)
                    for i in range(per):
                        last = pe.matmul(bank[2 * (u % 2) + i][:, :], weights(side)[i], xT[:, c * CH:(c + 1) * CH],
                                         start=True, stop=True)
                    last.then_inc(s["projected"], 1)
                for u in range(V_UNITS):
                    if u >= 2:
                        pe.wait_ge(s["v_taken"], u - 1)
                    for i in range(tiles_per_bank):
                        t = u * tiles_per_bank + i
                        last = pe.matmul(bank[4 + u % 2][:, i * width:(i + 1) * width], xT[:, t * P:(t + 1) * P],
                                         v_w, start=True, stop=True)
                    last.then_inc(s["v_done"], 1)

            @block.vector
            def _(dve):
                for u in range(UNITS):
                    side, c = unit(u)
                    j = u % 2
                    psum = bank[2 * j]
                    dve.wait_ge(s["projected"], u + 1)
                    if rope:
                        cos, sin = rope
                        cols = slice((c % 2) * CH, (c % 2 + 1) * CH)
                        w = weights(side)
                        dve.scalar_tensor_tensor(out=t1[:, j, :], in0=psum[:, :], scalar=w[2], in1=cos[:, cols],
                                                 op0=ALU.add, op1=ALU.mult).then_inc(s["rot1"], 1)
                        dve.scalar_tensor_tensor(out=t2[:, j, :], in0=bank[2 * j + 1][:, :], scalar=w[3],
                                                 in1=sin[:, cols], op0=ALU.add, op1=ALU.mult).then_inc(s["rot2"], 1)
                        dve.wait_ge(s["rot1"], u + 1)
                        dve.wait_ge(s["rot2"], u + 1)
                        dve.tensor_tensor(x32[:, j, :], t1[:, j, :], t2[:, j, :], ALU.add).then_inc(s["rotated"], 1)
                        source = x32[:, j, :]
                    else:
                        source = psum[:, :]
                    dve.wait_ge(s["high"], u + 1)
                    if u >= 2:
                        dve.wait_ge(s["mid"], u - 1)
                    dve.tensor_tensor(rest[:, j, :], source, parts[:, j, 0, :], ALU.subtract
                                      ).then_inc(s["minus_high"], 1)
                    dve.wait_ge(s["mid"], u + 1)
                    dve.tensor_tensor(parts[:, j, 2, :], rest[:, j, :], parts[:, j, 1, :], ALU.subtract
                                      ).then_inc(s["low"], 1)
                for u in range(V_UNITS):
                    dve.wait_ge(s["v_done"], u + 1)
                    t0 = u * tiles_per_bank
                    b, j0 = t0 // TPB, t0 % TPB
                    out = vt[:, b * GPB * TPB * HG * e_dim:(b + 1) * GPB * TPB * HG * e_dim].rearrange(
                        "p (g j c) -> p j g c", g=GPB, j=TPB)[:, j0:j0 + tiles_per_bank]
                    got = bank[4 + u % 2][:, :].rearrange("p (j g c) -> p j g c", j=tiles_per_bank, g=GPB)
                    if v_bias is None:
                        dve.tensor_copy(out, got).then_inc(s["v_taken"], 1)
                    else:
                        bias = v_bias.rearrange("p (g c) -> p g c", g=GPB).unsqueeze(1).to_broadcast(
                            [P, tiles_per_bank, GPB, HG * e_dim])
                        dve.tensor_tensor(out, got, bias, ALU.add).then_inc(s["v_taken"], 1)

            @block.scalar
            def _(act):
                for u in range(UNITS):
                    j = u % 2
                    act.wait_ge(s["rotated"] if rope else s["projected"], u + 1)
                    if u >= 2:
                        act.wait_ge(s[f"parts_out{j}"], 16 * (u // 2))
                    act.copy(parts[:, j, 0, :], x32[:, j, :] if rope else bank[2 * j][:, :]).then_inc(s["high"], 1)
                    act.wait_ge(s["minus_high"], u + 1)
                    act.copy(parts[:, j, 1, :], rest[:, j, :]).then_inc(s["mid"], 1)

            @block.sync
            def _(sync):
                if rezero:
                    pairs = qs[:, :].rearrange("p (j a t) -> p a j t", a=2, t=N)
                    for a in range(2):
                        mine, zero = HALF * a + MAXROW, HALF * (1 - a) + MAXROW
                        sync.dma_start(pairs[mine:mine + 2, a], pairs[zero:zero + 2, a]).then_inc(s["zeroed"], 16)
                for u in range(UNITS):
                    side, c = unit(u)
                    sync.wait_ge(s["low"], u + 1)
                    sync.dma_start(parts_dram[side, :, :, c * CH:(c + 1) * CH].rearrange("k p t -> p k t"),
                                   parts[:, u % 2, :, :]).then_inc(s[f"parts_out{u % 2}"], 16)
                    if c % 2 == 1:
                        sync.wait_ge(s[f"parts_out{u % 2}"], 16 * (u // 2 + 1))
                        b = c // 2
                        for i, (kp, qp) in enumerate(PRODUCTS):
                            for a in range(2):
                                row = HALF * a + DH * i
                                src = parts_dram[side, (qp, kp)[side], :, b * N:(b + 1) * N].rearrange(
                                    "(j a d) t -> a d j t", a=2, d=DH)[a]
                                if side == 0:
                                    dst = qs[row:row + DH, b * H * N:(b + 1) * H * N].rearrange(
                                        "d (j a t) -> d a j t", a=2, t=N)[:, a]
                                else:
                                    dst = ks[row:row + DH, b * (H // 2) * N:(b + 1) * (H // 2) * N].rearrange(
                                        "d (j t) -> d j t", t=N)
                                sync.dma_start(dst, src).then_inc(s["stacked"], 16)
                if rezero:
                    sync.wait_ge(s["zeroed"], 32)
                sync.wait_ge(s["stacked"], 16 * 2 * 2 * 2 * len(PRODUCTS))

        k.release()


def project_out(nc, kit, tag, o, e_dim, w, x, bank, ident):
    parts = e_dim * H // P
    with ExitStack() as life:
        k = Kit(nc, life)
        oT = k.sb(f"oT_{tag}", [P, 2, parts, CH])
        turned, copied = k.sem(f"o_turned2_{tag}"), k.sem(f"oT_copied_{tag}")
        projected, added = k.sem(f"o_projected_{tag}"), k.sem(f"o_added_{tag}")
        tiles = o[:, :].rearrange("p (t m c) -> p t m c", t=TILES, m=parts)
        with nc.Block() as block:

            @block.tensor
            def _(pe):
                def turn(c):
                    if c >= 2:
                        pe.wait_ge(copied, c - 1)
                    for i in range(TPC):
                        t = c * TPC + i
                        for m in range(parts):
                            last = pe.transpose(bank[(c % 2) * parts + m][:, i * P:(i + 1) * P], tiles[:, t, m, :],
                                                ident)
                    last.then_inc(turned, 1)

                def project(c):
                    pe.wait_ge(copied, c + 1)
                    if c >= 2:
                        pe.wait_ge(added, c - 1)
                    for i in range(TPC):
                        for m in range(parts):
                            last = pe.matmul(bank[4 + c % 2][:, i * P:(i + 1) * P], oT[:, c % 2, m, i * P:(i + 1) * P],
                                             w[m], start=(m == 0), stop=(m == parts - 1))
                    last.then_inc(projected, 1)

                turn(0)
                for c in range(CHUNKS):
                    if c + 1 < CHUNKS:
                        turn(c + 1)
                    project(c)

            @block.scalar
            def _(act):
                for c in range(CHUNKS):
                    act.wait_ge(turned, c + 1)
                    if c >= 2:
                        act.wait_ge(projected, c - 1)
                    for m in range(parts):
                        last = act.copy(oT[:, c % 2, m, :], bank[(c % 2) * parts + m][:, :])
                    last.then_inc(copied, 1)

            @block.vector
            def _(dve):
                for c in range(CHUNKS):
                    dve.wait_ge(projected, c + 1)
                    xc = x[:, c * TPC:(c + 1) * TPC, :].rearrange("p t d -> p (t d)")
                    dve.tensor_tensor(xc, bank[4 + c % 2][:, :], xc, ALU.add).then_inc(added, 1)
                dve.wait_ge(added, CHUNKS)

        k.release()


def experts(nc, kit, tag, x, xT, d, bank, ident):
    with ExitStack() as life:
        k = Kit(nc, life)
        w1 = k.sb(f"w1_{tag}", [P, E, FF])
        w2 = k.sb(f"w2_{tag}", [P, E, FC, D])
        b1 = k.sb(f"b1_{tag}", [P, E, FC])
        b2 = k.sb(f"b2_{tag}", [E, D])
        gw = k.sb(f"gw_{tag}", [P, E])
        h = k.sb(f"h_{tag}", [P, 2, FC, CH])
        logit = k.sb(f"logit_{tag}", [P, TILES, E])
        prob = k.sb(f"prob_{tag}", [P, TILES, E])
        first = k.sb(f"first_{tag}", [P, TILES, E])
        gate = k.sb(f"gate_{tag}", [P, TILES, E])
        rank = k.sb(f"rank_{tag}", [P, E])
        top = k.sb(f"top_{tag}", [P, 4, TILES])
        gateT = k.sb(f"gateT_{tag}", [E, TOK])
        names = ["gw_in", "b_in", "ranked", "routed", "shifted", "r_exp", "r_step", "gated", "g_turned", "g_copied",
                 "b2_done", "x_init", "hidden", "gelu", "y_done", "x_step"]
        s = {n: k.sem(f"{n}_{tag}") for n in names}
        w_in = [k.sem(f"w_in{e}_{tag}") for e in range(E)]
        hidden_bank = [bank[0:2], bank[2:4]]
        y_bank = bank[4:6]

        with nc.Block() as block:

            @block.sync
            def _(sync):
                sync.dma_start(gw[:, :], d["gate_w"]).then_inc(s["gw_in"], 16)
                sync.dma_start(b1[:, :, :], d["b1"]).then_inc(s["b_in"], 16)
                sync.dma_start(b2[:, :], d["b2"]).then_inc(s["b_in"], 16)
                for e in range(E):
                    sync.dma_start(w1[:, e, :], d["w1"][e]).then_inc(w_in[e], 16)
                    sync.dma_start(w2[:, e, :, :], d["w2"][e].rearrange("(c p) d -> p c d", p=P)).then_inc(w_in[e], 16)

            @block.tensor
            def _(pe):
                pe.wait_ge(s["gw_in"], 16)
                for t in range(TILES):
                    last = pe.matmul(bank[6][:, t * E:(t + 1) * E], xT[:, t * P:(t + 1) * P], gw[:, :],
                                     start=True, stop=True)
                last.then_inc(s["routed"], 1)

                def hidden(e, c):
                    kk = c * E + e
                    for half in range(2):
                        v = 2 * kk + half
                        if not (is_first(c) and e == 0):
                            pe.wait_ge(s["gelu"], v - 1)
                        for i in range(2):
                            f = 2 * half + i
                            last = pe.matmul(hidden_bank[half][i][:, :], w1[:, e, f * P:(f + 1) * P],
                                             xT[:, bass.ds(c * CH, CH)], start=True, stop=True)
                        last.then_inc(s["hidden"], 1)

                def down(e, c):
                    kk = c * E + e
                    pe.wait_ge(s["gelu"], 2 * (kk + 1))
                    if not (is_first(c) and e < 2):
                        pe.wait_ge(s["x_step"], (kk - 1) * TPC)
                    for i in range(TPC):
                        for f in range(FC):
                            last = pe.matmul(y_bank[e % 2][:, i * P:(i + 1) * P], h[:, e % 2, f, i * P:(i + 1) * P],
                                             w2[:, e, f, :], start=(f == 0), stop=(f == FC - 1))
                    last.then_inc(s["y_done"], 1)

                def chunk(c):
                    for e in range(E):
                        if is_first(c):
                            pe.wait_ge(w_in[e], 32)
                        hidden(e, c)
                        if e > 0:
                            down(e - 1, c)
                        elif not is_first(c):
                            down(E - 1, c - 1)

                def bias():
                    pe.wait_ge(s["b_in"], 32)
                    for c in range(CHUNKS):
                        if c == 0:
                            pe.wait_ge(s["gated"], 1)
                            pe.wait_ge(s["shifted"], 1)
                        else:
                            pe.wait_ge(s["g_copied"], c)
                        for i in range(TPC):
                            last = pe.transpose(bank[6][0:E, i * P:(i + 1) * P], gate[:, c * TPC + i, :], ident)
                        last.then_inc(s["g_turned"], 1)
                    for c in range(CHUNKS):
                        pe.wait_ge(s["g_copied"], c + 1)
                        if c > 0:
                            pe.wait_ge(s["x_init"], c)
                        for i in range(TPC):
                            t = c * TPC + i
                            last = pe.matmul(bank[7][:, i * P:(i + 1) * P], gateT[:, t * P:(t + 1) * P], b2[:, :],
                                             start=True, stop=True)
                        last.then_inc(s["b2_done"], 1)

                for e in range(2):
                    pe.wait_ge(w_in[e], 32)
                    hidden(e, 0)
                    if e == 0:
                        bias()
                        down(0, 0)
                for e in range(2, E):
                    pe.wait_ge(w_in[e], 32)
                    hidden(e, 0)
                    down(e - 1, 0)
                with pe.Fori(1, CHUNKS) as c:
                    chunk(c)
                down(E - 1, CHUNKS - 1)

            @block.scalar
            def _(act):
                act.wait_ge(s["shifted"], 1)
                act.activation(prob[:, :, :], logit[:, :, :], ACT.Exp).then_inc(s["r_exp"], 1)
                act.wait_ge(s["b_in"], 32)

                def chunk(c):
                    for e in range(E):
                        kk = c * E + e
                        for half in range(2):
                            act.wait_ge(s["hidden"], 2 * kk + half + 1)
                            if not (is_first(c) and e < 2):
                                act.wait_ge(s["y_done"], kk - 1)
                            for i in range(2):
                                f = 2 * half + i
                                last = act.activation(h[:, e % 2, f, :], hidden_bank[half][i][:, :], ACT.Gelu,
                                                      bias=b1[:, e, f:f + 1])
                            last.then_inc(s["gelu"], 1)

                chunk(0)
                with act.Fori(1, CHUNKS) as c:
                    chunk(c)

            @block.vector
            def _(dve):
                shape = [P, TILES, E]
                over = lambda i: top[:, i, :].unsqueeze(2).to_broadcast(shape)
                for e in range(E):
                    dve.memset(rank[:, e:e + 1], float(E - e)).then_inc(s["ranked"], 1)
                dve.wait_ge(s["routed"], 1)
                got = bank[6][:, 0:TILES * E].rearrange("p (t e) -> p t e", e=E)
                steps = 0

                def done(ins):
                    nonlocal steps
                    steps += 1
                    ins.then_inc(s["r_step"], 1)
                    dve.wait_ge(s["r_step"], steps)

                done(dve.tensor_reduce(top[:, 0, :], got, AX, ALU.max))
                dve.tensor_tensor(logit[:, :, :], got, over(0), ALU.subtract).then_inc(s["shifted"], 1)
                dve.wait_ge(s["r_exp"], 1)
                done(dve.tensor_reduce(top[:, 1, :], prob[:, :, :], AX, ALU.add))
                done(dve.reciprocal(top[:, 2, :], top[:, 1, :]))
                done(dve.tensor_tensor(prob[:, :, :], prob[:, :, :], over(2), ALU.mult))
                done(dve.tensor_reduce(top[:, 3, :], prob[:, :, :], AX, ALU.max))
                done(dve.tensor_tensor(first[:, :, :], prob[:, :, :], over(3), ALU.is_equal))
                dve.wait_ge(s["ranked"], E)
                done(dve.tensor_tensor(first[:, :, :], first[:, :, :],
                                       rank[:, :].unsqueeze(1).to_broadcast(shape), ALU.mult))
                done(dve.tensor_reduce(top[:, 0, :], first[:, :, :], AX, ALU.max))
                done(dve.tensor_tensor(gate[:, :, :], first[:, :, :], over(0), ALU.is_equal))
                dve.tensor_tensor(gate[:, :, :], gate[:, :, :], over(3), ALU.mult).then_inc(s["gated"], 1)
                dve.wait_ge(s["gated"], 1)
                for c in range(CHUNKS):
                    dve.wait_ge(s["g_turned"], c + 1)
                    dve.tensor_copy(gateT[:, c * CH:(c + 1) * CH], bank[6][0:E, :]).then_inc(s["g_copied"], 1)
                for c in range(CHUNKS):
                    dve.wait_ge(s["b2_done"], c + 1)
                    xc = x[:, c * TPC:(c + 1) * TPC, :].rearrange("p t d -> p (t d)")
                    dve.tensor_tensor(xc, bank[7][:, :], xc, ALU.add).then_inc(s["x_init"], 1)
                dve.wait_ge(s["x_init"], CHUNKS)

                def chunk(c):
                    for e in range(E):
                        kk = c * E + e
                        dve.wait_ge(s["y_done"], kk + 1)
                        if not (is_first(c) and e == 0):
                            dve.wait_ge(s["x_step"], kk * TPC)
                        for i in range(TPC):
                            xt = xf[:, bass.ds((c * TPC + i) * D, D)]
                            dve.scalar_tensor_tensor(out=xt, in0=y_bank[e % 2][:, i * P:(i + 1) * P],
                                                     scalar=gf[:, bass.ds((c * TPC + i) * E + e, 1)], in1=xt,
                                                     op0=ALU.mult, op1=ALU.add).then_inc(s["x_step"], 1)

                xf = x[:, :, :].rearrange("p t d -> p (t d)")
                gf = gate[:, :, :].rearrange("p t e -> p (t e)")
                chunk(0)
                with dve.Fori(1, CHUNKS) as c:
                    chunk(c)
                dve.wait_ge(s["x_step"], CHUNKS * E * TPC)

        k.release()


def batchnorm(nc, kit, xT, xb, gamma, beta):
    with ExitStack() as life:
        k = Kit(nc, life)
        stats = k.sb("bn_stats", [P, CHUNKS, 6])
        mv = k.sb("bn_mv", [P, 2])
        sc = k.sb("bn_sc", [P, 4])
        chain, std_done = k.sem("bn_chain"), k.sem("bn_std_done")
        with nc.Block() as block:

            @block.vector
            def _(dve):
                for c in range(CHUNKS):
                    dve.bn_stats(stats[:, c, :], xT[:, c * CH:(c + 1) * CH]).then_inc(chain, 1)
                dve.wait_ge(chain, CHUNKS)
                dve.bn_aggr(mv[:, :], stats[:, :, :].rearrange("p c s -> p (c s)")).then_inc(chain, 1)
                dve.wait_ge(std_done, 1)
                dve.reciprocal(sc[:, 1:2], sc[:, 0:1]).then_inc(chain, 1)
                dve.wait_ge(chain, CHUNKS + 2)
                dve.tensor_tensor(sc[:, 2:3], sc[:, 1:2], gamma, ALU.mult).then_inc(chain, 1)
                dve.wait_ge(chain, CHUNKS + 3)
                dve.tensor_scalar(sc[:, 3:4], mv[:, 0:1], sc[:, 2:3], -1.0, ALU.mult, ALU.mult).then_inc(chain, 1)
                dve.wait_ge(chain, CHUNKS + 4)
                dve.tensor_tensor(sc[:, 3:4], sc[:, 3:4], beta, ALU.add).then_inc(chain, 1)
                dve.wait_ge(chain, CHUNKS + 5)
                for c in range(CHUNKS):
                    dve.tensor_scalar(xb[:, c * CH:(c + 1) * CH], xT[:, c * CH:(c + 1) * CH], sc[:, 2:3], sc[:, 3:4],
                                      ALU.mult, ALU.add).then_inc(chain, 1)
                dve.wait_ge(chain, 2 * CHUNKS + 5)

            @block.scalar
            def _(act):
                act.wait_ge(chain, CHUNKS + 1)
                act.activation(sc[:, 0:1], mv[:, 1:2], ACT.Sqrt, bias=LN_EPS).then_inc(std_done, 1)

        k.release()


def divide_plain(dve, num, rec, where, tmp, q, s):
    dve.tensor_tensor(where.rearrange("p i (h e) -> p i h e", h=HG), num, rec, ALU.mult).then_inc(s["turn_read"], 1)


def make_divide_difference(neg_lam):
    def step(dve, num, rec, where, tmp, q, s):
        dve.tensor_tensor(tmp[:, :, :, :], num, rec, ALU.mult).then_inc(s["turn_read"], 1)
        dve.wait_ge(s["turn_read"], q + 1)
        dve.scalar_tensor_tensor(out=where, in0=tmp[:, :, :, :].rearrange("p i h e -> p i (h e)"),
                                 scalar=neg_lam, in1=where, op0=ALU.mult, op1=ALU.add
                                 ).then_inc(s["o_done"], 1)
    return step


def hybrid_kernel(nc, d, out):
    with ExitStack() as life:
        kit = Kit(nc, life)
        bank = [life.enter_context(nc.psum_tensor(f"bank{i}", [P, CH], F32)) for i in range(8)]
        x = kit.sb("x", [P, TILES, D])
        xT = kit.sb("xT", [P, TOK])
        qs = kit.sb("query_stacks", [P, B * H * N], BF16)
        ks = kit.sb("key_stacks", [P, B * H // 2 * N], BF16)
        identt = kit.sb("ident", [P, P])
        identbt = kit.sb("identb", [P, P], BF16)
        ident, identb = identt[:, :], identbt[:, :]
        parts_dram = nc.dram_tensor("parts_dram", [2, 3, P, TOK], BF16, kind="Internal").ap()

        x_in, cleared, ident_in = kit.sem("x_in"), kit.sem("cleared"), kit.sem("ident_in")
        with nc.Block() as block:

            @block.sync
            def _(sync):
                for b in range(B):
                    sync.dma_start(x[:, b * TPB:(b + 1) * TPB, :],
                                   d["x"][b].rearrange("(p t) d -> p t d", t=TPB)).then_inc(x_in, 16)
                sync.dma_start(ident, d["ident"]).then_inc(ident_in, 16)
                sync.wait_ge(x_in, 32)

            @block.vector
            def _(dve):
                dve.wait_ge(ident_in, 16)
                dve.tensor_copy(identb, ident).then_inc(cleared, 1)
                n = B * H * N // 2
                dve.memset(qs[:, 0:n].bitcast(F32), 0.0).then_inc(cleared, 1)

            @block.gpsimd
            def _(pool):
                n = B * H * N // 2
                pool.memset(qs[:, n:2 * n].bitcast(F32), 0.0).then_inc(cleared, 1)

            @block.scalar
            def _(act):
                pass

        cleared2 = kit.sem("cleared_keys")
        with nc.Block() as block:

            @block.vector
            def _(dve):
                for a in range(2):
                    row = HALF * a + HALF // 2
                    dve.memset(ks[row:row + HALF // 2, :], 1.0).then_inc(cleared2, 1)

        layernorm_transposed(nc, kit, "ln0", x, xT, bank, ident)

        with ExitStack() as phase:
            k = Kit(nc, phase)
            cos, sin = k.sb("cos", [P, N]), k.sb("sin", [P, N])
            wa = k.sb("wa", [P, 6, D])
            ba = k.sb("ba", [P, 4])
            bvo = k.sb("bvo", [P, 2, D])
            vt = k.sb("vt_a", [P, GROUPS * TPB * HG * DH])
            o = k.sb("o_a", [P, GROUPS * TPB * HG * DH])
            a_in, o_biased = kit.sem("a_in"), kit.sem("o_biased")
            with nc.Block() as block:

                @block.sync
                def _(sync):
                    n = 0
                    sync.dma_start(cos[:, :], d["cos"]).then_inc(a_in, 16)
                    sync.dma_start(sin[:, :], d["sin"]).then_inc(a_in, 16)
                    for i, w in enumerate(["WqT", "WqT2", "WkT", "WkT2", "WvT", "WoT"]):
                        sync.dma_start(wa[:, i, :], d[w]).then_inc(a_in, 16)
                    for i, w in enumerate(["bq", "bq2", "bk", "bk2"]):
                        sync.dma_start(ba[:, i:i + 1], d[w].unsqueeze(1)).then_inc(a_in, 16)
                    for i, w in enumerate(["bv", "bo"]):
                        sync.dma_start(bvo[:, i, :], d[w].partition_broadcast(P)).then_inc(a_in, 16)
                    sync.wait_ge(a_in, 16 * 14)

                @block.gpsimd
                def _(pool):
                    pool.wait_ge(a_in, 16 * 14)
                    pool.tensor_tensor(x[:, :, :], x[:, :, :], bvo[:, 1, :].unsqueeze(1).to_broadcast([P, TILES, D]),
                                       ALU.add).then_inc(o_biased, 1)

            prepare(nc, kit, "a", xT, [wa[:, 0, :], wa[:, 1, :], ba[:, 0:1], ba[:, 1:2]],
                    [wa[:, 2, :], wa[:, 3, :], ba[:, 2:3], ba[:, 3:4]],
                    (wa[:, 4, :], vt, bvo[:, 0, :], DH), parts_dram, qs, ks, bank, rope=(cos, sin))
            attention(nc, kit, "a", qs, ks, vt, o, bank, ident, identb, DH, divide_plain)
            project_out(nc, kit, "a", o, DH, [wa[:, 5, :]], x, bank, ident)

        layernorm_transposed(nc, kit, "ln1", x, xT, bank, ident)
        experts(nc, kit, "f1", x, xT, d, bank, ident)
        layernorm_transposed(nc, kit, "ln2", x, xT, bank, ident)

        with ExitStack() as phase:
            k = Kit(nc, phase)
            EB = 2 * DH
            wb = k.sb("wb", [P, 4, D])
            wv = k.sb("wv", [P, 2 * D])
            wc = k.sb("wc", [P, 2, D])
            cols = k.sb("cols", [P, 3])
            lams = k.sb("lams", [P, 4, DH])
            lamp = k.sb("lamp", [P, 2, DH])
            lamv = k.sb("lamv", [P, 6])
            vt = k.sb("vt_b", [P, GROUPS * TPB * HG * EB])
            o = k.sb("o_b", [P, GROUPS * TPB * HG * EB])
            b_in, lam_chain, lam_exp, wc_done = (kit.sem(n) for n in ["b_in", "lam_chain", "lam_exp", "wc_done"])
            with nc.Block() as block:

                @block.sync
                def _(sync):
                    for i, w in enumerate(["q1T", "k1T", "q2T", "k2T"]):
                        sync.dma_start(wb[:, i, :], d[w]).then_inc(b_in, 16)
                    sync.dma_start(wv[:, :], d["vT"]).then_inc(b_in, 16)
                    sync.dma_start(wc[:, :, :], d["cT"].rearrange("(m p) n -> p m n", p=P)).then_inc(b_in, 16)
                    for i, w in enumerate(["gamma", "beta", "subln"]):
                        sync.dma_start(cols[:, i:i + 1], d[w].unsqueeze(1)).then_inc(b_in, 16)
                    for i, w in enumerate(["lq1", "lk1", "lq2", "lk2"]):
                        sync.dma_start(lams[:, i, :], d[w].partition_broadcast(P)).then_inc(b_in, 16)
                    sync.wait_ge(b_in, 16 * 13)

                @block.vector
                def _(dve):
                    dve.wait_ge(b_in, 16 * 13)
                    for i in range(2):
                        dve.tensor_tensor(lamp[:, i, :], lams[:, 2 * i, :], lams[:, 2 * i + 1, :], ALU.mult
                                          ).then_inc(lam_chain, 1)
                    dve.wait_ge(lam_chain, 2)
                    dve.tensor_reduce(lamv[:, 0:2], lamp[:, :, :], AX, ALU.add).then_inc(lam_chain, 1)
                    dve.tensor_scalar(wc[:, :, :], wc[:, :, :], cols[:, 2:3], 1.0 - LAMBDA_INIT, ALU.mult, ALU.mult
                                      ).then_inc(wc_done, 1)
                    dve.wait_ge(lam_exp, 1)
                    dve.tensor_tensor(lamv[:, 4:5], lamv[:, 3:4], lamv[:, 2:3], ALU.subtract).then_inc(lam_chain, 1)
                    dve.wait_ge(lam_chain, 4)
                    dve.tensor_scalar(lamv[:, 5:6], lamv[:, 4:5], -LAMBDA_INIT, None, ALU.add).then_inc(lam_chain, 1)
                    dve.wait_ge(lam_chain, 5)

                @block.scalar
                def _(act):
                    act.wait_ge(lam_chain, 3)
                    act.activation(lamv[:, 2:4], lamv[:, 0:2], ACT.Exp).then_inc(lam_exp, 1)

            batchnorm(nc, kit, xT, xT, cols[:, 0:1], cols[:, 1:2])
            prepare(nc, kit, "b1", xT, [wb[:, 0, :]], [wb[:, 1, :]], (wv[:, :], vt, None, EB), parts_dram, qs, ks,
                    bank, rezero=True)
            attention(nc, kit, "b1", qs, ks, vt, o, bank, ident, identb, EB, divide_plain)
            prepare(nc, kit, "b2", xT, [wb[:, 2, :]], [wb[:, 3, :]], (wv[:, :], vt, None, EB), parts_dram, qs, ks,
                    bank, rezero=True)
            attention(nc, kit, "b2", qs, ks, vt, o, bank, ident, identb, EB,
                      make_divide_difference(lamv[:, 5:6]))

            sq, ms = k.sb("sq", [P, H * EB]), k.sb("ms", [P, 2, TILES * H])
            squared, summed, rooted, inverted, scaled = (
                kit.sem(n) for n in ["squared", "summed", "rooted", "inverted", "scaled"])
            rows = GROUPS * TPB * HG
            PIECE = rows // TILES
            with nc.Block() as block:

                @block.vector
                def _(dve):
                    for i in range(TILES):
                        piece = o[:, i * PIECE * EB:(i + 1) * PIECE * EB]
                        if i > 0:
                            dve.wait_ge(summed, i)
                        dve.tensor_tensor(sq[:, :], piece, piece, ALU.mult).then_inc(squared, 1)
                        dve.wait_ge(squared, i + 1)
                        dve.tensor_reduce(ms[:, 0, i * PIECE:(i + 1) * PIECE],
                                          sq[:, :].rearrange("p (r e) -> p r e", e=EB), AX, ALU.add
                                          ).then_inc(summed, 1)
                    dve.wait_ge(rooted, 1)
                    dve.reciprocal(ms[:, 0, :], ms[:, 1, :]).then_inc(inverted, 1)
                    dve.wait_ge(inverted, 1)
                    all_o = o[:, :].rearrange("p (r e) -> p r e", e=EB)
                    dve.tensor_tensor(all_o, all_o, ms[:, 0, :].unsqueeze(2).to_broadcast([P, rows, EB]), ALU.mult
                                      ).then_inc(scaled, 1)
                    dve.wait_ge(scaled, 1)

                @block.scalar
                def _(act):
                    act.wait_ge(summed, TILES)
                    act.activation(ms[:, 1, :], ms[:, 0, :], ACT.Sqrt, bias=LN_EPS, scale=1.0 / EB
                                   ).then_inc(rooted, 1)

            project_out(nc, kit, "b", o, EB, [wc[:, 0, :], wc[:, 1, :]], x, bank, ident)

        layernorm_transposed(nc, kit, "ln3", x, xT, bank, ident)
        experts(nc, kit, "f2", x, xT, d, bank, ident)

        stored = kit.sem("stored")
        with nc.Block() as block:

            @block.sync
            def _(sync):
                for b in range(B):
                    sync.dma_start(out[b].rearrange("(p t) d -> p t d", t=TPB),
                                   x[:, b * TPB:(b + 1) * TPB, :]).then_inc(stored, 16)
                sync.wait_ge(stored, 32)


def constants():
    inv = (1.0 / 10000.0 ** (np.arange(0, DH, 2, dtype=np.float32) / DH)).astype(np.float32)
    pos = (np.arange(P)[None, :] * TPB + np.arange(TPB)[:, None]).reshape(-1).astype(np.float32)
    theta = (pos[None, :] * inv[:, None]).astype(np.float32)
    row = (np.arange(P) % DH) // 2
    sign = np.where(np.arange(P) % 2 == 0, -1.0, 1.0).astype(np.float32)
    return {"cos": np.cos(theta).astype(np.float32)[row],
            "sin": (np.sin(theta).astype(np.float32)[row] * sign[:, None]).astype(np.float32),
            "ident": np.eye(P, dtype=np.float32)}


def kernel(**inputs):
    import concourse.bacc as bacc
    from concourse.bass_utils import run_bass_kernel_spmd

    g = {n: np.asarray(v) for n, v in inputs.items()}
    other = np.arange(P) ^ 1
    a, b, f = "L0_attn_a_", "L0_attn_b_", "L0_ffn_"
    arrays = {
        "x": g[a + "x"],
        "WqT": g[a + "Wq"].T, "WqT2": g[a + "Wq"][other].T, "WkT": g[a + "Wk"].T, "WkT2": g[a + "Wk"][other].T,
        "WvT": g[a + "Wv"].T, "WoT": g[a + "Wo"].T,
        "bq": g[a + "bq"], "bq2": g[a + "bq"][other], "bk": g[a + "bk"], "bk2": g[a + "bk"][other],
        "bv": g[a + "bv"], "bo": g[a + "bo"],
        "q1T": g[b + "q1_w"].T, "k1T": g[b + "k1_w"].T, "q2T": g[b + "q2_w"].T, "k2T": g[b + "k2_w"].T,
        "vT": g[b + "v_w"].T, "cT": g[b + "c_w"].T,
        "gamma": g[b + "bn_gamma"], "beta": g[b + "bn_beta"], "subln": np.tile(g[b + "subln_w"], P // (2 * DH)),
        "lq1": g[b + "lq1"], "lk1": g[b + "lk1"], "lq2": g[b + "lq2"], "lk2": g[b + "lk2"],
        "gate_w": g[f + "gate_w"], "w1": g[f + "w1"], "b1": g[f + "b1"].reshape(E, FC, P).transpose(2, 0, 1), "w2": g[f + "w2"], "b2": g[f + "b2"],
        **constants(),
    }
    nc = bacc.Bacc("TRN2", target_bir_lowering=False, num_devices=1)
    named, d = {}, {}
    for name, v in arrays.items():
        v = np.ascontiguousarray(v)
        named[f"in_{name}"] = v
        d[name] = nc.dram_tensor(f"in_{name}", v.shape, mybir.dt.from_np(v.dtype), kind="ExternalInput").ap()
    out = nc.dram_tensor("out_x", (B, N, D), F32, kind="ExternalOutput").ap()
    hybrid_kernel(nc, d, out)
    r = run_bass_kernel_spmd(nc, [named], core_ids=[0])
    return r.results[0]["out_x"]
```

```python
import math
from contextlib import ExitStack

import numpy as np
import concourse.bass as bass
from concourse import mybir

F32 = mybir.dt.float32
BF16 = mybir.dt.bfloat16
ACT = mybir.ActivationFunctionType
ALU = mybir.AluOpType
AX = mybir.AxisListType.X

P = 128
B, N, D = 2, 1024, 128
TOK = B * N
TPB = N // P
TILES = TOK // P
CH = 512
CHUNKS = TOK // CH
TPC = CH // P
H, DH = 16, 8
HG = 4
GPB = H // HG
GROUPS = B * GPB
VC = 32
E, FF = 8, 512
FC = FF // P
LN_EPS = 1e-5
LAMBDA_INIT = 0.8 - 0.6 * math.exp(-0.3)
SCALE = 1.0 / math.sqrt(DH)

PRODUCTS = [(0, 0), (0, 1), (1, 0), (1, 1), (0, 2), (2, 0)]
HALF = 64
MAXROW = DH * len(PRODUCTS)


def is_first(g):
    return isinstance(g, int) and g == 0


class Kit:

    def __init__(self, nc, life):
        self.nc, self.life, self.sems = nc, life, []

    def sb(self, name, shape, dtype=F32):
        return self.life.enter_context(self.nc.sbuf_tensor(name, shape, dtype))

    def sem(self, name):
        self.sems.append(self.nc.alloc_semaphore(name))
        return self.sems[-1]

    def release(self):
        self.nc.clear_and_free_semaphores(self.sems)
        self.nc.all_engine_barrier()


def layernorm_transposed(nc, tag, x, xT, bank, ident, extra_loads=None):
    with ExitStack() as life:
        k = Kit(nc, life)
        stats = k.sb(f"stats_{tag}", [P, TILES, 6])
        mv = k.sb(f"mv_{tag}", [P, TILES, 2])
        std = k.sb(f"std_{tag}", [P, TILES])
        rstd = k.sb(f"rstd_{tag}", [P, TILES])
        xn = k.sb(f"xn_{tag}", [P, TILES, D])
        stats_done, mv_done = k.sem(f"stats_done_{tag}"), k.sem(f"mv_done_{tag}")
        std_done, rstd_done = k.sem(f"std_done_{tag}"), k.sem(f"rstd_done_{tag}")
        xn_done, turned = k.sem(f"xn_done_{tag}"), k.sem(f"turned_{tag}")
        copied = k.sem(f"copied_{tag}")
        with nc.Block() as block:

            @block.vector
            def _(dve):
                for t in range(TILES):
                    dve.bn_stats(stats[:, t, :], x[:, t, :]).then_inc(stats_done, 1)
                dve.wait_ge(stats_done, TILES)
                for t in range(TILES):
                    dve.bn_aggr(mv[:, t, :], stats[:, t, :]).then_inc(mv_done, 1)
                dve.wait_ge(std_done, 1)
                dve.reciprocal(rstd[:, :], std[:, :]).then_inc(rstd_done, 1)
                dve.wait_ge(rstd_done, 1)
                for t in range(TILES):
                    dve.tensor_scalar(xn[:, t, :], x[:, t, :], mv[:, t, 0:1], rstd[:, t:t + 1],
                                      ALU.subtract, ALU.mult).then_inc(xn_done, 1)

            @block.scalar
            def _(act):
                act.wait_ge(mv_done, TILES)
                act.activation(std[:, :], mv[:, :, 1], ACT.Sqrt, bias=LN_EPS).then_inc(std_done, 1)
                for c in range(CHUNKS):
                    act.wait_ge(turned, c + 1)
                    act.copy(xT[:, c * CH:(c + 1) * CH], bank[c % 2][:, :]).then_inc(copied, 1)
                act.wait_ge(copied, CHUNKS)

            @block.tensor
            def _(pe):
                for c in range(CHUNKS):
                    pe.wait_ge(xn_done, TPC * (c + 1))
                    if c >= 2:
                        pe.wait_ge(copied, c - 1)
                    for i in range(TPC):
                        last = pe.transpose(bank[c % 2][:, i * P:(i + 1) * P], xn[:, c * TPC + i, :], ident)
                    last.then_inc(turned, 1)

        k.release()


def attention(nc, tag, maps, qs, ks, vt, o, bank, ident, identb, e_dim, neg_lam, refill):
    STEPS = TPB
    LEAD = 4
    QT = TPC
    LAST = (maps - 1, GROUPS - 1, 1)
    ALL = maps * GROUPS * 2

    def count(pos):
        m, g, half = pos
        return (m * GROUPS + g) * 2 + half

    def is_at(pos, where):
        return isinstance(pos[1], int) and pos == where

    def is_first(pos):
        return is_at(pos, (0, 0, 0))

    def after(pos):
        m, g, half = pos
        if is_at(pos, LAST):
            return None
        if half == 0:
            return (m, g, 1)
        return (m + 1, 0, 0) if isinstance(g, int) and g == GROUPS - 1 else (m, g + 1, 0)

    def bank_free(i):
        previous = i - 3 if i >= 3 else max(j for j in range(STEPS * HG) if j % 3 == i % 3) - STEPS * HG
        return previous + 1 - i

    def tiles_before(engine, pos, step):
        m, g, half = pos
        base = (m * GROUPS + g) * (2 * STEPS * HG)
        more = (half * STEPS + step) * HG
        if isinstance(g, int):
            return base + more
        with engine.register(f"tiles_{tag}_{nc.next_id()}") as tiles:
            engine.reg_add(tiles, base, more)
            return engine.snap(tiles)

    def everything(engine, half_group, refilled=None):
        for m in range(maps):
            for half in range(2):
                half_group((m, 0, half))
            if m == 1 and refilled is not None:
                spans = [(1, GPB - 1), (GPB - 1, GROUPS - 1)]
            else:
                spans = [(1, GROUPS - 1)]
            for n, (start, end) in enumerate(spans):
                if n == 1:
                    engine.wait_ge(refilled, refill.total)
                with engine.Fori(start, end) as g:
                    for half in range(2):
                        half_group((m, g, half))
            for half in range(2):
                half_group((m, GROUPS - 1, half))

    with ExitStack() as life:
        k = Kit(nc, life)
        vs = k.sb(f"vs_{tag}", [P, TPB, HG, VC])
        probs = k.sb(f"probs_{tag}", [P, 2, HG, CH])
        ots = k.sb(f"ots_{tag}", [P, CH])
        mx = k.sb(f"mx_{tag}", [P, HG, QT, 2])
        nmax = k.sb(f"nmax_{tag}", [P, QT, HG])
        nmaxb = k.sb(f"nmaxb_{tag}", [P, QT, HG, 2], BF16)
        maxrows = k.sb(f"maxrows_{tag}", [HG * 2, CH], BF16)
        rec = k.sb(f"rec_{tag}", [P, QT, HG])
        tmp = k.sb(f"tmp_{tag}", [P, QT, HG, e_dim])
        names = ["max_scored", "max_taken", "max_joined", "max_split", "max_turned", "max_copied",
                 "max_rows", "scored", "exped", "multiplied", "v_ones", "v_staged", "o_copied",
                 "o_turned", "turn_read", "o_rec", "o_done", "refilled0", "refilled1"]
        s = {n: k.sem(f"{n}_{tag}") for n in names}
        score_bank, max_bank = bank[0:3], bank[3:6]
        out_bank, turn_bank = bank[6], bank[7]
        turnb = turn_bank[:, :].bitcast(BF16)

        def q_from(g, first):
            return g * (HG * N) + first

        def k_from(g, first):
            return g * (HG // 2 * N) + first

        def q_at(column, h, n):
            return qs[:, bass.ds(column + h * N, n)]

        def k_at(column, h, n):
            return ks[:, bass.ds(column + (h // 2) * N, n)]

        with nc.Block() as block:

            @block.tensor
            def _(pe):
                def max_scores(pos, step):
                    m, g, half = pos
                    if step == 0 and is_at(pos, (1, 0, 0)):
                        pe.wait_ge(s["refilled0"], refill.total)
                    tiles = tiles_before(pe, pos, step)
                    queries = q_from(g, half * CH + (step // 2) * P)
                    keys = k_from(g, (step % 2) * CH)

                    def one(h):
                        i = step * HG + h
                        if not (is_first(pos) and i < 3):
                            pe.wait_ge(s["max_taken"], tiles + h + bank_free(i))
                        pe.matmul(max_bank[i % 3][:, :], q_at(queries, h, P), k_at(keys, h, CH),
                                  start=True, stop=True).then_inc(s["max_scored"], 1)
                    return one

                def turn_max(pos):
                    pe.wait_ge(s["max_split"], 2 * (count(pos) + 1))
                    if not is_first(pos) and not is_at(pos, (0, 0, 1)):
                        pe.wait_ge(s["turn_read"], count(pos) - 1)
                    for j in range(QT):
                        last = pe.transpose(turnb[0:HG * 2, j * P:(j + 1) * P],
                                            nmaxb[:, j, :, :].rearrange("p h c -> p (h c)"), identb)
                    last.then_inc(s["max_turned"], 1)

                def scores(pos, step):
                    m, g, half = pos
                    tiles = tiles_before(pe, pos, step)
                    keys = k_from(g, step * P)
                    queries = q_from(g, half * CH)
                    if step == 0:
                        pe.wait_ge(s["max_rows"], 16 * HG * (count(pos) + 1))

                    def one(h):
                        i = step * HG + h
                        if not (is_first(pos) and i < 3):
                            pe.wait_ge(s["exped"], tiles + h + bank_free(i))
                        pe.matmul(score_bank[i % 3][:, :], k_at(keys, h, P), q_at(queries, h, CH),
                                  start=True, stop=True).then_inc(s["scored"], 1)
                    return one

                def multiply(pos, step):
                    m, g, half = pos
                    pe.wait_ge(s["exped"], HG * (count(pos) * STEPS + step + 1))
                    if half == 0 and step == 0:
                        pe.wait_ge(s["v_staged"], 2 * (m * GROUPS + g) + 1)
                    if half == 0 and step == TPB - 1:
                        pe.wait_ge(s["v_staged"], 2 * (m * GROUPS + g) + 2)
                    if step == 0 and not is_first(pos):
                        pe.wait_ge(s["o_copied"], count(pos))
                    for h in range(HG):
                        last = pe.matmul(out_bank[VC * h:VC * (h + 1), :], vs[:, step, h, :],
                                         probs[:, step % 2, h, :],
                                         start=(step == 0), stop=(step == STEPS - 1))
                    last.then_inc(s["multiplied"], 1)

                def turn_out(pos):
                    n = count(pos)
                    pe.wait_ge(s["o_copied"], n + 1)
                    if is_at(pos, LAST):
                        pe.wait_ge(s["turn_read"], n)
                    else:
                        pe.wait_ge(s["max_copied"], n + 2)
                    for i in range(QT):
                        last = pe.transpose(turn_bank[:, i * P:(i + 1) * P], ots[:, i * P:(i + 1) * P], ident)
                    last.then_inc(s["o_turned"], 1)

                before = None

                def half_group(pos):
                    nonlocal before
                    nxt = after(pos)
                    nxt2 = after(nxt) if nxt else None
                    if not is_first(pos):
                        m, g, half = pos
                        before = (m, g, 0) if half else ((m - 1, GROUPS - 1, 1) if isinstance(g, int) and g == 0
                                                         else (m, g - 1, 1))
                    for step in range(STEPS):
                        ahead, where = (step + LEAD, nxt) if step + LEAD < STEPS else (step + LEAD - STEPS, nxt2)
                        score = scores(pos, step)
                        max_score = max_scores(where, ahead) if where else None
                        for h in range(HG):
                            score(h)
                            if max_score:
                                max_score(h)
                        if step > 0:
                            multiply(pos, step - 1)
                        elif before:
                            multiply(before, STEPS - 1)
                        if step == 1 and before:
                            turn_out(before)
                        if step == STEPS - LEAD and nxt:
                            turn_max(nxt)

                for step in range(STEPS):
                    for h in range(HG):
                        max_scores((0, 0, 0), step)(h)
                turn_max((0, 0, 0))
                for step in range(LEAD):
                    for h in range(HG):
                        max_scores((0, 0, 1), step)(h)
                everything(pe, half_group, s["refilled1"])
                multiply(LAST, STEPS - 1)
                turn_out(LAST)

            @block.scalar
            def _(act):
                def exponentials(pos, step):
                    tiles = tiles_before(act, pos, step)
                    for h in range(HG):
                        i = step * HG + h
                        act.wait_ge(s["scored"], tiles + h + 1)
                        if h == 0 and not (is_first(pos) and step < 2):
                            act.wait_ge(s["multiplied"], count(pos) * STEPS + step - 1)
                        act.activation(probs[:, step % 2, h, :], score_bank[i % 3][:, :], ACT.Exp, scale=SCALE
                                       ).then_inc(s["exped"], 1)

                def copy_out(n, first=False):
                    act.wait_ge(s["multiplied"], TPB * (n + 1))
                    if not first:
                        act.wait_ge(s["o_turned"], n)
                    act.copy(ots[:, :], out_bank[:, :]).then_inc(s["o_copied"], 1)

                def copy_max(n, first=False):
                    act.wait_ge(s["max_turned"], n + 1)
                    if not first:
                        act.wait_ge(s["max_rows"], 16 * HG * n)
                    act.copy(maxrows[:, :], turnb[0:HG * 2, 0:CH]).then_inc(s["max_copied"], 1)

                def half_group(pos):
                    n = count(pos)
                    for step in range(STEPS):
                        exponentials(pos, step)
                        if step == 0 and not is_first(pos):
                            copy_out(n - 1, first=is_at(pos, (0, 0, 1)))
                        if step == STEPS - LEAD + 1 and not is_at(pos, LAST):
                            copy_max(n + 1)

                copy_max(0, first=True)
                everything(act, half_group)
                copy_out(ALL - 1)

            @block.vector
            def _(dve):
                def take_max(pos, step):
                  tiles = tiles_before(dve, pos, step)
                  for h in range(HG):
                    dve.wait_ge(s["max_scored"], tiles + h + 1)
                    dve.tensor_reduce(mx[:, h, step // 2, step % 2:step % 2 + 1], max_bank[(step * HG + h) % 3][:, :],
                                      AX, ALU.max).then_inc(s["max_taken"], 1)

                def split_max(pos):
                    n = count(pos)
                    dve.wait_ge(s["max_taken"], HG * STEPS * (n + 1))
                    if not is_first(pos):
                        dve.wait_ge(s["max_turned"], n)
                    dve.tensor_tensor(nmax[:, :, :].rearrange("p j h -> p h j"), mx[:, :, :, 0], mx[:, :, :, 1],
                                      ALU.max).then_inc(s["max_joined"], 1)
                    dve.wait_ge(s["max_joined"], n + 1)
                    dve.tensor_scalar(nmaxb[:, :, :, 0], nmax[:, :, :], -1.0, None, ALU.mult
                                      ).then_inc(s["max_split"], 1)
                    dve.wait_ge(s["max_split"], 2 * n + 1)
                    dve.scalar_tensor_tensor(out=nmaxb[:, :, :, 1], in0=nmax[:, :, :], scalar=-1.0,
                                             in1=nmaxb[:, :, :, 0], op0=ALU.mult, op1=ALU.subtract
                                             ).then_inc(s["max_split"], 1)

                def divide(pos):
                    m, g, half = pos
                    n = count(pos)
                    tiles = o[:, :].rearrange("p (t w) -> p t w", t=TILES)
                    where = tiles[:, bass.ds((g // GPB) * TPB + half * TPC, TPC),
                                  bass.ds((g % GPB) * HG * e_dim, HG * e_dim)]
                    dve.wait_ge(s["o_turned"], n + 1)
                    t = turn_bank[:, :].rearrange("p (i h c) -> p i h c", i=QT, h=HG)
                    dve.reciprocal(rec[:, :, :], t[:, :, :, e_dim]).then_inc(s["o_rec"], 1)
                    dve.wait_ge(s["o_rec"], n + 1)
                    r = rec[:, :, :].unsqueeze(3).to_broadcast([P, QT, HG, e_dim])
                    if m == 0:
                        dve.tensor_tensor(where.rearrange("p i (h e) -> p i h e", h=HG), t[:, :, :, 0:e_dim], r,
                                          ALU.mult).then_inc(s["turn_read"], 1)
                    else:
                        dve.tensor_tensor(tmp[:, :, :, :], t[:, :, :, 0:e_dim], r, ALU.mult
                                          ).then_inc(s["turn_read"], 1)
                        dve.wait_ge(s["turn_read"], n + 1)
                        dve.scalar_tensor_tensor(out=where, in0=tmp[:, :, :, :].rearrange("p i h e -> p i (h e)"),
                                                 scalar=neg_lam, in1=where, op0=ALU.mult, op1=ALU.add
                                                 ).then_inc(s["o_done"], 1)

                def half_group(pos):
                    nxt = after(pos)
                    nxt2 = after(nxt) if nxt else None
                    m, g, half = pos
                    if half:
                        before = (m, g, 0)
                    elif isinstance(g, int) and g == 0:
                        before = (m - 1, GROUPS - 1, 1) if m else None
                    else:
                        before = (m, g - 1, 1)
                    for step in range(STEPS):
                        ahead, where = (step + LEAD, nxt) if step + LEAD < STEPS else (step + LEAD - STEPS, nxt2)
                        if where:
                            take_max(where, ahead)
                        if ahead == STEPS - 1 and nxt:
                            split_max(nxt)
                        if step == 1 and before:
                            divide(before)

                for step in range(STEPS):
                    take_max((0, 0, 0), step)
                split_max((0, 0, 0))
                for step in range(LEAD):
                    take_max((0, 0, 1), step)
                everything(dve, half_group)
                divide(LAST)

            @block.gpsimd
            def _(pool):
                pool.memset(vs[:, :, :, :], 1.0).then_inc(s["v_ones"], 1)
                pool.wait_ge(s["v_ones"], 1)

                def stage(m, g):
                    n = m * GROUPS + g
                    v = vt[:, bass.ds(g * TPB * HG * e_dim, TPB * HG * e_dim)].rearrange(
                        "p (j h e) -> p j h e", j=TPB, h=HG)
                    first = m == 0 and isinstance(g, int) and g == 0
                    if not first:
                        pool.wait_ge(s["multiplied"], n * 2 * STEPS - 1)
                    pool.tensor_copy(vs[:, 0:TPB - 1, :, 0:e_dim], v[:, 0:TPB - 1]).then_inc(s["v_staged"], 1)
                    if not first:
                        pool.wait_ge(s["multiplied"], n * 2 * STEPS)
                    pool.tensor_copy(vs[:, TPB - 1, :, 0:e_dim], v[:, TPB - 1]).then_inc(s["v_staged"], 1)

                for m in range(maps):
                    stage(m, 0)
                    with pool.Fori(1, GROUPS) as g:
                        stage(m, g)

            @block.sync
            def _(sync):
                def write_max(pos):
                    m, g, half = pos
                    sync.wait_ge(s["max_copied"], count(pos) + 1)
                    for h in range(HG):
                        row = HALF * (h % 2) + MAXROW
                        sync.dma_start(qs[row:row + 2, bass.ds((g * HG + h) * N + half * CH, CH)],
                                       maxrows[2 * h:2 * h + 2, :]).then_inc(s["max_rows"], 16)

                def refill_batch(b):
                    sync.wait_ge(s["scored"], (b + 1) * GPB * 2 * STEPS * HG)
                    refill.start(sync, b, s[f"refilled{b}"])

                for m in range(maps):
                    for half in range(2):
                        write_max((m, 0, half))
                        if m == 1 and half == 0:
                            refill_batch(1)
                    with sync.Fori(1, GPB) as g:
                        for half in range(2):
                            write_max((m, g, half))
                    write_max((m, GPB, 0))
                    if maps == 2 and m == 0:
                        refill_batch(0)
                    write_max((m, GPB, 1))
                    with sync.Fori(GPB + 1, GROUPS) as g:
                        for half in range(2):
                            write_max((m, g, half))
                sync.wait_ge(s["max_rows"], 16 * HG * ALL)
                if maps == 2:
                    sync.wait_ge(s["refilled1"], refill.total)

        k.release()


def stack_side(sync, parts, side, b, qs, ks, done):
    for i, (kp, qp) in enumerate(PRODUCTS):
        for a in range(2):
            row = HALF * a + DH * i
            src = parts[side, (qp, kp)[side], :, b * N:(b + 1) * N].rearrange("(j a d) t -> a d j t", a=2, d=DH)[a]
            if side == 0:
                dst = qs[row:row + DH, b * H * N:(b + 1) * H * N].rearrange("d (j a t) -> d a j t", a=2, t=N)[:, a]
            else:
                dst = ks[row:row + DH, b * (H // 2) * N:(b + 1) * (H // 2) * N].rearrange("d (j t) -> d j t", t=N)
            sync.dma_start(dst, src).then_inc(done, 16)


def clear_maxima(sync, b, qs, done):
    pairs = qs[:, b * H * N:(b + 1) * H * N].rearrange("p (j a t) -> p a j t", a=2, t=N)
    for a in range(2):
        mine, zero = HALF * a + MAXROW, HALF * (1 - a) + MAXROW
        sync.dma_start(pairs[mine:mine + 2, a], pairs[zero:zero + 2, a]).then_inc(done, 16)


class Refill:

    total = 16 * (2 + 2 * 2 * len(PRODUCTS))

    def __init__(self, parts, qs, ks):
        self.parts, self.qs, self.ks = parts, qs, ks

    def start(self, sync, b, done):
        clear_maxima(sync, b, self.qs, done)
        for side in range(2):
            stack_side(sync, self.parts, side, b, self.qs, self.ks, done)


def prepare(nc, tag, xT, sides, v, parts_dram, qs, ks, bank, rope=None, rezero=False):
    UNITS = len(sides) * CHUNKS
    with ExitStack() as life:
        k = Kit(nc, life)
        parts = k.sb(f"parts_{tag}", [P, 2, 3, CH], BF16)
        rest = k.sb(f"rest_{tag}", [P, 2, CH])
        x32 = k.sb(f"x32_{tag}", [P, 2, CH]) if rope else None
        t1 = k.sb(f"t1_{tag}", [P, 2, CH]) if rope else None
        t2 = k.sb(f"t2_{tag}", [P, 2, CH]) if rope else None
        names = ["projected", "rot1", "rot2", "rotated", "high", "minus_high", "mid", "low", "parts_out0", "parts_out1",
                 "stacked", "zeroed", "v_done", "v_taken"]
        s = {n: k.sem(f"{n}_{tag}") for n in names}
        per = 2 if rope else 1
        unit = lambda u: (u // (2 * CHUNKS) * 2 + u % 2, u // 2 % CHUNKS)
        weights = lambda side: sides[side]
        v_w, vt, v_bias, e_dim = v
        width = H * e_dim
        tiles_per_bank = CH // width
        V_UNITS = TILES // tiles_per_bank

        with nc.Block() as block:

            @block.tensor
            def _(pe):
                for u in range(UNITS):
                    side, c = unit(u)
                    if u >= 2:
                        pe.wait_ge(s["rot2"] if rope else s["minus_high"], u - 1)
                    for i in range(per):
                        last = pe.matmul(bank[2 * (u % 2) + i][:, :], weights(side)[i], xT[:, c * CH:(c + 1) * CH],
                                         start=True, stop=True)
                    last.then_inc(s["projected"], 1)
                for u in range(V_UNITS):
                    if u >= 2:
                        pe.wait_ge(s["v_taken"], u - 1)
                    for i in range(tiles_per_bank):
                        t = u * tiles_per_bank + i
                        last = pe.matmul(bank[4 + u % 2][:, i * width:(i + 1) * width], xT[:, t * P:(t + 1) * P],
                                         v_w, start=True, stop=True)
                    last.then_inc(s["v_done"], 1)

            @block.vector
            def _(dve):
                for u in range(UNITS):
                    side, c = unit(u)
                    j = u % 2
                    psum = bank[2 * j]
                    dve.wait_ge(s["projected"], u + 1)
                    if rope:
                        cos, sin = rope
                        cols = slice((c % 2) * CH, (c % 2 + 1) * CH)
                        w = weights(side)
                        dve.scalar_tensor_tensor(out=t1[:, j, :], in0=psum[:, :], scalar=w[2], in1=cos[:, cols],
                                                 op0=ALU.add, op1=ALU.mult).then_inc(s["rot1"], 1)
                        dve.scalar_tensor_tensor(out=t2[:, j, :], in0=bank[2 * j + 1][:, :], scalar=w[3],
                                                 in1=sin[:, cols], op0=ALU.add, op1=ALU.mult).then_inc(s["rot2"], 1)
                        dve.wait_ge(s["rot1"], u + 1)
                        dve.wait_ge(s["rot2"], u + 1)
                        dve.tensor_tensor(x32[:, j, :], t1[:, j, :], t2[:, j, :], ALU.add).then_inc(s["rotated"], 1)
                        source = x32[:, j, :]
                    else:
                        source = psum[:, :]
                    dve.wait_ge(s["high"], u + 1)
                    if u >= 2:
                        dve.wait_ge(s["mid"], u - 1)
                    dve.tensor_tensor(rest[:, j, :], source, parts[:, j, 0, :], ALU.subtract
                                      ).then_inc(s["minus_high"], 1)
                    dve.wait_ge(s["mid"], u + 1)
                    dve.tensor_tensor(parts[:, j, 2, :], rest[:, j, :], parts[:, j, 1, :], ALU.subtract
                                      ).then_inc(s["low"], 1)
                for u in range(V_UNITS):
                    dve.wait_ge(s["v_done"], u + 1)
                    t0 = u * tiles_per_bank
                    b, j0 = t0 // TPB, t0 % TPB
                    out = vt[:, b * GPB * TPB * HG * e_dim:(b + 1) * GPB * TPB * HG * e_dim].rearrange(
                        "p (g j c) -> p j g c", g=GPB, j=TPB)[:, j0:j0 + tiles_per_bank]
                    got = bank[4 + u % 2][:, :].rearrange("p (j g c) -> p j g c", j=tiles_per_bank, g=GPB)
                    if v_bias is None:
                        dve.tensor_copy(out, got).then_inc(s["v_taken"], 1)
                    else:
                        bias = v_bias.rearrange("p (g c) -> p g c", g=GPB).unsqueeze(1).to_broadcast(
                            [P, tiles_per_bank, GPB, HG * e_dim])
                        dve.tensor_tensor(out, got, bias, ALU.add).then_inc(s["v_taken"], 1)

            @block.scalar
            def _(act):
                for u in range(UNITS):
                    j = u % 2
                    act.wait_ge(s["rotated"] if rope else s["projected"], u + 1)
                    if u >= 2:
                        act.wait_ge(s[f"parts_out{j}"], 16 * (u // 2))
                    act.copy(parts[:, j, 0, :], x32[:, j, :] if rope else bank[2 * j][:, :]).then_inc(s["high"], 1)
                    act.wait_ge(s["minus_high"], u + 1)
                    act.copy(parts[:, j, 1, :], rest[:, j, :]).then_inc(s["mid"], 1)

            @block.sync
            def _(sync):
                if rezero:
                    for b in range(B):
                        clear_maxima(sync, b, qs, s["zeroed"])
                for u in range(UNITS):
                    side, c = unit(u)
                    sync.wait_ge(s["low"], u + 1)
                    dram = parts_dram[side // 2]
                    sync.dma_start(dram[side % 2, :, :, c * CH:(c + 1) * CH].rearrange("k p t -> p k t"),
                                   parts[:, u % 2, :, :]).then_inc(s[f"parts_out{u % 2}"], 16)
                    if c % 2 == 1 and side < 2:
                        sync.wait_ge(s[f"parts_out{u % 2}"], 16 * (u // 2 + 1))
                        stack_side(sync, dram, side, c // 2, qs, ks, s["stacked"])
                for side in range(2):
                    sync.wait_ge(s[f"parts_out{side}"], 16 * (UNITS // 2))
                if rezero:
                    sync.wait_ge(s["zeroed"], 16 * 2 * B)
                sync.wait_ge(s["stacked"], 16 * 2 * 2 * 2 * len(PRODUCTS))

        k.release()


def project_out(nc, tag, o, e_dim, w, x, bank, ident):
    parts = e_dim * H // P
    with ExitStack() as life:
        k = Kit(nc, life)
        oT = k.sb(f"oT_{tag}", [P, 2, parts, CH])
        turned, copied = k.sem(f"o_turned2_{tag}"), k.sem(f"oT_copied_{tag}")
        projected, added = k.sem(f"o_projected_{tag}"), k.sem(f"o_added_{tag}")
        tiles = o[:, :].rearrange("p (t m c) -> p t m c", t=TILES, m=parts)
        with nc.Block() as block:

            @block.tensor
            def _(pe):
                def turn(c):
                    if c >= 2:
                        pe.wait_ge(copied, c - 1)
                    for i in range(TPC):
                        t = c * TPC + i
                        for m in range(parts):
                            last = pe.transpose(bank[(c % 2) * parts + m][:, i * P:(i + 1) * P], tiles[:, t, m, :],
                                                ident)
                    last.then_inc(turned, 1)

                def project(c):
                    pe.wait_ge(copied, c + 1)
                    if c >= 2:
                        pe.wait_ge(added, c - 1)
                    for i in range(TPC):
                        for m in range(parts):
                            last = pe.matmul(bank[4 + c % 2][:, i * P:(i + 1) * P], oT[:, c % 2, m, i * P:(i + 1) * P],
                                             w[m], start=(m == 0), stop=(m == parts - 1))
                    last.then_inc(projected, 1)

                turn(0)
                for c in range(CHUNKS):
                    if c + 1 < CHUNKS:
                        turn(c + 1)
                    project(c)

            @block.scalar
            def _(act):
                for c in range(CHUNKS):
                    act.wait_ge(turned, c + 1)
                    if c >= 2:
                        act.wait_ge(projected, c - 1)
                    for m in range(parts):
                        last = act.copy(oT[:, c % 2, m, :], bank[(c % 2) * parts + m][:, :])
                    last.then_inc(copied, 1)

            @block.vector
            def _(dve):
                for c in range(CHUNKS):
                    dve.wait_ge(projected, c + 1)
                    xc = x[:, c * TPC:(c + 1) * TPC, :].rearrange("p t d -> p (t d)")
                    dve.tensor_tensor(xc, bank[4 + c % 2][:, :], xc, ALU.add).then_inc(added, 1)
                dve.wait_ge(added, CHUNKS)

        k.release()


def experts(nc, tag, x, xT, d, bank, ident):
    with ExitStack() as life:
        k = Kit(nc, life)
        w1 = k.sb(f"w1_{tag}", [P, E, FF])
        w2 = k.sb(f"w2_{tag}", [P, E, FC, D])
        b1 = k.sb(f"b1_{tag}", [P, E, FC])
        b2 = k.sb(f"b2_{tag}", [E, D])
        gw = k.sb(f"gw_{tag}", [P, E])
        h = k.sb(f"h_{tag}", [P, 2, FC, CH])
        logit = k.sb(f"logit_{tag}", [P, TILES, E])
        prob = k.sb(f"prob_{tag}", [P, TILES, E])
        first = k.sb(f"first_{tag}", [P, TILES, E])
        gate = k.sb(f"gate_{tag}", [P, TILES, E])
        rank = k.sb(f"rank_{tag}", [P, E])
        top = k.sb(f"top_{tag}", [P, 4, TILES])
        gateT = k.sb(f"gateT_{tag}", [E, TOK])
        names = ["gw_in", "b_in", "ranked", "routed", "shifted", "r_exp", "r_step", "gated", "g_turned", "g_copied",
                 "b2_done", "x_init", "hidden", "gelu", "y_done", "x_step"]
        s = {n: k.sem(f"{n}_{tag}") for n in names}
        w_in = [k.sem(f"w_in{e}_{tag}") for e in range(E)]
        hidden_bank = [bank[0:2], bank[2:4]]
        y_bank = bank[4:6]

        with nc.Block() as block:

            @block.sync
            def _(sync):
                sync.dma_start(gw[:, :], d["gate_w"]).then_inc(s["gw_in"], 16)
                sync.dma_start(b1[:, :, :], d["b1"]).then_inc(s["b_in"], 16)
                sync.dma_start(b2[:, :], d["b2"]).then_inc(s["b_in"], 16)
                for e in range(E):
                    sync.dma_start(w1[:, e, :], d["w1"][e]).then_inc(w_in[e], 16)
                    sync.dma_start(w2[:, e, :, :], d["w2"][e].rearrange("(c p) d -> p c d", p=P)).then_inc(w_in[e], 16)

            @block.tensor
            def _(pe):
                pe.wait_ge(s["gw_in"], 16)
                for t in range(TILES):
                    last = pe.matmul(bank[6][:, t * E:(t + 1) * E], xT[:, t * P:(t + 1) * P], gw[:, :],
                                     start=True, stop=True)
                last.then_inc(s["routed"], 1)

                def hidden(e, c):
                    kk = c * E + e
                    for half in range(2):
                        v = 2 * kk + half
                        if not (is_first(c) and e == 0):
                            pe.wait_ge(s["gelu"], v - 1)
                        for i in range(2):
                            f = 2 * half + i
                            last = pe.matmul(hidden_bank[half][i][:, :], w1[:, e, f * P:(f + 1) * P],
                                             xT[:, bass.ds(c * CH, CH)], start=True, stop=True)
                        last.then_inc(s["hidden"], 1)

                def down(e, c):
                    kk = c * E + e
                    pe.wait_ge(s["gelu"], 2 * (kk + 1))
                    if not (is_first(c) and e < 2):
                        pe.wait_ge(s["x_step"], (kk - 1) * TPC)
                    for i in range(TPC):
                        for f in range(FC):
                            last = pe.matmul(y_bank[e % 2][:, i * P:(i + 1) * P], h[:, e % 2, f, i * P:(i + 1) * P],
                                             w2[:, e, f, :], start=(f == 0), stop=(f == FC - 1))
                    last.then_inc(s["y_done"], 1)

                def chunk(c):
                    for e in range(E):
                        if is_first(c):
                            pe.wait_ge(w_in[e], 32)
                        hidden(e, c)
                        if e > 0:
                            down(e - 1, c)
                        elif not is_first(c):
                            down(E - 1, c - 1)

                def bias():
                    pe.wait_ge(s["b_in"], 32)
                    for c in range(CHUNKS):
                        if c == 0:
                            pe.wait_ge(s["gated"], 1)
                            pe.wait_ge(s["shifted"], 1)
                        else:
                            pe.wait_ge(s["g_copied"], c)
                        for i in range(TPC):
                            last = pe.transpose(bank[6][0:E, i * P:(i + 1) * P], gate[:, c * TPC + i, :], ident)
                        last.then_inc(s["g_turned"], 1)
                    for c in range(CHUNKS):
                        pe.wait_ge(s["g_copied"], c + 1)
                        if c > 0:
                            pe.wait_ge(s["x_init"], c)
                        for i in range(TPC):
                            t = c * TPC + i
                            last = pe.matmul(bank[7][:, i * P:(i + 1) * P], gateT[:, t * P:(t + 1) * P], b2[:, :],
                                             start=True, stop=True)
                        last.then_inc(s["b2_done"], 1)

                for e in range(2):
                    pe.wait_ge(w_in[e], 32)
                    hidden(e, 0)
                    if e == 0:
                        bias()
                        down(0, 0)
                for e in range(2, E):
                    pe.wait_ge(w_in[e], 32)
                    hidden(e, 0)
                    down(e - 1, 0)
                with pe.Fori(1, CHUNKS) as c:
                    chunk(c)
                down(E - 1, CHUNKS - 1)

            @block.scalar
            def _(act):
                act.wait_ge(s["shifted"], 1)
                act.activation(prob[:, :, :], logit[:, :, :], ACT.Exp).then_inc(s["r_exp"], 1)
                act.wait_ge(s["b_in"], 32)

                def chunk(c):
                    for e in range(E):
                        kk = c * E + e
                        for half in range(2):
                            act.wait_ge(s["hidden"], 2 * kk + half + 1)
                            if not (is_first(c) and e < 2):
                                act.wait_ge(s["y_done"], kk - 1)
                            for i in range(2):
                                f = 2 * half + i
                                last = act.activation(h[:, e % 2, f, :], hidden_bank[half][i][:, :], ACT.Gelu,
                                                      bias=b1[:, e, f:f + 1])
                            last.then_inc(s["gelu"], 1)

                chunk(0)
                with act.Fori(1, CHUNKS) as c:
                    chunk(c)

            @block.vector
            def _(dve):
                shape = [P, TILES, E]
                over = lambda i: top[:, i, :].unsqueeze(2).to_broadcast(shape)
                for e in range(E):
                    dve.memset(rank[:, e:e + 1], float(E - e)).then_inc(s["ranked"], 1)
                dve.wait_ge(s["routed"], 1)
                got = bank[6][:, 0:TILES * E].rearrange("p (t e) -> p t e", e=E)
                steps = 0

                def done(ins):
                    nonlocal steps
                    steps += 1
                    ins.then_inc(s["r_step"], 1)
                    dve.wait_ge(s["r_step"], steps)

                done(dve.tensor_reduce(top[:, 0, :], got, AX, ALU.max))
                dve.tensor_tensor(logit[:, :, :], got, over(0), ALU.subtract).then_inc(s["shifted"], 1)
                dve.wait_ge(s["r_exp"], 1)
                done(dve.tensor_reduce(top[:, 1, :], prob[:, :, :], AX, ALU.add))
                done(dve.reciprocal(top[:, 2, :], top[:, 1, :]))
                done(dve.tensor_tensor(prob[:, :, :], prob[:, :, :], over(2), ALU.mult))
                done(dve.tensor_reduce(top[:, 3, :], prob[:, :, :], AX, ALU.max))
                done(dve.tensor_tensor(first[:, :, :], prob[:, :, :], over(3), ALU.is_equal))
                dve.wait_ge(s["ranked"], E)
                done(dve.tensor_tensor(first[:, :, :], first[:, :, :],
                                       rank[:, :].unsqueeze(1).to_broadcast(shape), ALU.mult))
                done(dve.tensor_reduce(top[:, 0, :], first[:, :, :], AX, ALU.max))
                done(dve.tensor_tensor(gate[:, :, :], first[:, :, :], over(0), ALU.is_equal))
                dve.tensor_tensor(gate[:, :, :], gate[:, :, :], over(3), ALU.mult).then_inc(s["gated"], 1)
                dve.wait_ge(s["gated"], 1)
                for c in range(CHUNKS):
                    dve.wait_ge(s["g_turned"], c + 1)
                    dve.tensor_copy(gateT[:, c * CH:(c + 1) * CH], bank[6][0:E, :]).then_inc(s["g_copied"], 1)
                for c in range(CHUNKS):
                    dve.wait_ge(s["b2_done"], c + 1)
                    xc = x[:, c * TPC:(c + 1) * TPC, :].rearrange("p t d -> p (t d)")
                    dve.tensor_tensor(xc, bank[7][:, :], xc, ALU.add).then_inc(s["x_init"], 1)
                dve.wait_ge(s["x_init"], CHUNKS)

                def chunk(c):
                    for e in range(E):
                        kk = c * E + e
                        dve.wait_ge(s["y_done"], kk + 1)
                        if not (is_first(c) and e == 0):
                            dve.wait_ge(s["x_step"], kk * TPC)
                        for i in range(TPC):
                            xt = xf[:, bass.ds((c * TPC + i) * D, D)]
                            dve.scalar_tensor_tensor(out=xt, in0=y_bank[e % 2][:, i * P:(i + 1) * P],
                                                     scalar=gf[:, bass.ds((c * TPC + i) * E + e, 1)], in1=xt,
                                                     op0=ALU.mult, op1=ALU.add).then_inc(s["x_step"], 1)

                xf = x[:, :, :].rearrange("p t d -> p (t d)")
                gf = gate[:, :, :].rearrange("p t e -> p (t e)")
                chunk(0)
                with dve.Fori(1, CHUNKS) as c:
                    chunk(c)
                dve.wait_ge(s["x_step"], CHUNKS * E * TPC)

        k.release()


def batchnorm(nc, xT, xb, gamma, beta):
    with ExitStack() as life:
        k = Kit(nc, life)
        stats = k.sb("bn_stats", [P, CHUNKS, 6])
        mv = k.sb("bn_mv", [P, 2])
        sc = k.sb("bn_sc", [P, 4])
        chain, std_done = k.sem("bn_chain"), k.sem("bn_std_done")
        with nc.Block() as block:

            @block.vector
            def _(dve):
                for c in range(CHUNKS):
                    dve.bn_stats(stats[:, c, :], xT[:, c * CH:(c + 1) * CH]).then_inc(chain, 1)
                dve.wait_ge(chain, CHUNKS)
                dve.bn_aggr(mv[:, :], stats[:, :, :].rearrange("p c s -> p (c s)")).then_inc(chain, 1)
                dve.wait_ge(std_done, 1)
                dve.reciprocal(sc[:, 1:2], sc[:, 0:1]).then_inc(chain, 1)
                dve.wait_ge(chain, CHUNKS + 2)
                dve.tensor_tensor(sc[:, 2:3], sc[:, 1:2], gamma, ALU.mult).then_inc(chain, 1)
                dve.wait_ge(chain, CHUNKS + 3)
                dve.tensor_scalar(sc[:, 3:4], mv[:, 0:1], sc[:, 2:3], -1.0, ALU.mult, ALU.mult).then_inc(chain, 1)
                dve.wait_ge(chain, CHUNKS + 4)
                dve.tensor_tensor(sc[:, 3:4], sc[:, 3:4], beta, ALU.add).then_inc(chain, 1)
                dve.wait_ge(chain, CHUNKS + 5)
                for c in range(CHUNKS):
                    dve.tensor_scalar(xb[:, c * CH:(c + 1) * CH], xT[:, c * CH:(c + 1) * CH], sc[:, 2:3], sc[:, 3:4],
                                      ALU.mult, ALU.add).then_inc(chain, 1)
                dve.wait_ge(chain, 2 * CHUNKS + 5)

            @block.scalar
            def _(act):
                act.wait_ge(chain, CHUNKS + 1)
                act.activation(sc[:, 0:1], mv[:, 1:2], ACT.Sqrt, bias=LN_EPS).then_inc(std_done, 1)

        k.release()


def hybrid_kernel(nc, d, out):
    with ExitStack() as life:
        kit = Kit(nc, life)
        bank = [life.enter_context(nc.psum_tensor(f"bank{i}", [P, CH], F32)) for i in range(8)]
        x = kit.sb("x", [P, TILES, D])
        xT = kit.sb("xT", [P, TOK])
        qs = kit.sb("query_stacks", [P, B * H * N], BF16)
        ks = kit.sb("key_stacks", [P, B * H // 2 * N], BF16)
        identt = kit.sb("ident", [P, P])
        identbt = kit.sb("identb", [P, P], BF16)
        ident, identb = identt[:, :], identbt[:, :]
        parts_dram = nc.dram_tensor("parts_dram", [2, 2, 3, P, TOK], BF16, kind="Internal").ap()

        x_in, cleared, ident_in = kit.sem("x_in"), kit.sem("cleared"), kit.sem("ident_in")
        with nc.Block() as block:

            @block.sync
            def _(sync):
                for b in range(B):
                    sync.dma_start(x[:, b * TPB:(b + 1) * TPB, :],
                                   d["x"][b].rearrange("(p t) d -> p t d", t=TPB)).then_inc(x_in, 16)
                sync.dma_start(ident, d["ident"]).then_inc(ident_in, 16)
                sync.wait_ge(x_in, 32)

            @block.vector
            def _(dve):
                dve.wait_ge(ident_in, 16)
                dve.tensor_copy(identb, ident).then_inc(cleared, 1)
                n = B * H * N // 2
                dve.memset(qs[:, 0:n].bitcast(F32), 0.0).then_inc(cleared, 1)

            @block.gpsimd
            def _(pool):
                n = B * H * N // 2
                pool.memset(qs[:, n:2 * n].bitcast(F32), 0.0).then_inc(cleared, 1)

            @block.scalar
            def _(act):
                pass

        cleared2 = kit.sem("cleared_keys")
        with nc.Block() as block:

            @block.vector
            def _(dve):
                for a in range(2):
                    row = HALF * a + HALF // 2
                    dve.memset(ks[row:row + HALF // 2, :], 1.0).then_inc(cleared2, 1)

        layernorm_transposed(nc, "ln0", x, xT, bank, ident)

        with ExitStack() as phase:
            k = Kit(nc, phase)
            cos, sin = k.sb("cos", [P, N]), k.sb("sin", [P, N])
            wa = k.sb("wa", [P, 6, D])
            ba = k.sb("ba", [P, 4])
            bvo = k.sb("bvo", [P, 2, D])
            vt = k.sb("vt_a", [P, GROUPS * TPB * HG * DH])
            o = k.sb("o_a", [P, GROUPS * TPB * HG * DH])
            a_in, o_biased = kit.sem("a_in"), kit.sem("o_biased")
            with nc.Block() as block:

                @block.sync
                def _(sync):
                    n = 0
                    sync.dma_start(cos[:, :], d["cos"]).then_inc(a_in, 16)
                    sync.dma_start(sin[:, :], d["sin"]).then_inc(a_in, 16)
                    for i, w in enumerate(["WqT", "WqT2", "WkT", "WkT2", "WvT", "WoT"]):
                        sync.dma_start(wa[:, i, :], d[w]).then_inc(a_in, 16)
                    for i, w in enumerate(["bq", "bq2", "bk", "bk2"]):
                        sync.dma_start(ba[:, i:i + 1], d[w].unsqueeze(1)).then_inc(a_in, 16)
                    for i, w in enumerate(["bv", "bo"]):
                        sync.dma_start(bvo[:, i, :], d[w].partition_broadcast(P)).then_inc(a_in, 16)
                    sync.wait_ge(a_in, 16 * 14)

                @block.gpsimd
                def _(pool):
                    pool.wait_ge(a_in, 16 * 14)
                    pool.tensor_tensor(x[:, :, :], x[:, :, :], bvo[:, 1, :].unsqueeze(1).to_broadcast([P, TILES, D]),
                                       ALU.add).then_inc(o_biased, 1)

            prepare(nc, "a", xT, [[wa[:, 0, :], wa[:, 1, :], ba[:, 0:1], ba[:, 1:2]],
                                  [wa[:, 2, :], wa[:, 3, :], ba[:, 2:3], ba[:, 3:4]]],
                    (wa[:, 4, :], vt, bvo[:, 0, :], DH), parts_dram, qs, ks, bank, rope=(cos, sin))
            attention(nc, "a", 1, qs, ks, vt, o, bank, ident, identb, DH, None, None)
            project_out(nc, "a", o, DH, [wa[:, 5, :]], x, bank, ident)

        layernorm_transposed(nc, "ln1", x, xT, bank, ident)
        experts(nc, "f1", x, xT, d, bank, ident)
        layernorm_transposed(nc, "ln2", x, xT, bank, ident)

        with ExitStack() as phase:
            k = Kit(nc, phase)
            EB = 2 * DH
            wb = k.sb("wb", [P, 4, D])
            wv = k.sb("wv", [P, 2 * D])
            wc = k.sb("wc", [P, 2, D])
            cols = k.sb("cols", [P, 3])
            lams = k.sb("lams", [P, 4, DH])
            lamp = k.sb("lamp", [P, 2, DH])
            lamv = k.sb("lamv", [P, 6])
            vt = k.sb("vt_b", [P, GROUPS * TPB * HG * EB])
            o = k.sb("o_b", [P, GROUPS * TPB * HG * EB])
            b_in, lam_chain, lam_exp, wc_done = (kit.sem(n) for n in ["b_in", "lam_chain", "lam_exp", "wc_done"])
            with nc.Block() as block:

                @block.sync
                def _(sync):
                    for i, w in enumerate(["q1T", "k1T", "q2T", "k2T"]):
                        sync.dma_start(wb[:, i, :], d[w]).then_inc(b_in, 16)
                    sync.dma_start(wv[:, :], d["vT"]).then_inc(b_in, 16)
                    sync.dma_start(wc[:, :, :], d["cT"].rearrange("(m p) n -> p m n", p=P)).then_inc(b_in, 16)
                    for i, w in enumerate(["gamma", "beta", "subln"]):
                        sync.dma_start(cols[:, i:i + 1], d[w].unsqueeze(1)).then_inc(b_in, 16)
                    for i, w in enumerate(["lq1", "lk1", "lq2", "lk2"]):
                        sync.dma_start(lams[:, i, :], d[w].partition_broadcast(P)).then_inc(b_in, 16)
                    sync.wait_ge(b_in, 16 * 13)

                @block.vector
                def _(dve):
                    dve.wait_ge(b_in, 16 * 13)
                    for i in range(2):
                        dve.tensor_tensor(lamp[:, i, :], lams[:, 2 * i, :], lams[:, 2 * i + 1, :], ALU.mult
                                          ).then_inc(lam_chain, 1)
                    dve.wait_ge(lam_chain, 2)
                    dve.tensor_reduce(lamv[:, 0:2], lamp[:, :, :], AX, ALU.add).then_inc(lam_chain, 1)
                    dve.tensor_scalar(wc[:, :, :], wc[:, :, :], cols[:, 2:3], 1.0 - LAMBDA_INIT, ALU.mult, ALU.mult
                                      ).then_inc(wc_done, 1)
                    dve.wait_ge(lam_exp, 1)
                    dve.tensor_tensor(lamv[:, 4:5], lamv[:, 3:4], lamv[:, 2:3], ALU.subtract).then_inc(lam_chain, 1)
                    dve.wait_ge(lam_chain, 4)
                    dve.tensor_scalar(lamv[:, 5:6], lamv[:, 4:5], -LAMBDA_INIT, None, ALU.add).then_inc(lam_chain, 1)
                    dve.wait_ge(lam_chain, 5)

                @block.scalar
                def _(act):
                    act.wait_ge(lam_chain, 3)
                    act.activation(lamv[:, 2:4], lamv[:, 0:2], ACT.Exp).then_inc(lam_exp, 1)

            batchnorm(nc, xT, xT, cols[:, 0:1], cols[:, 1:2])
            prepare(nc, "b", xT, [[wb[:, i, :]] for i in range(4)], (wv[:, :], vt, None, EB), parts_dram, qs, ks,
                    bank, rezero=True)
            attention(nc, "b", 2, qs, ks, vt, o, bank, ident, identb, EB, lamv[:, 5:6],
                      Refill(parts_dram[1], qs, ks))

            sq, ms = k.sb("sq", [P, H * EB]), k.sb("ms", [P, 2, TILES * H])
            squared, summed, rooted, inverted, scaled = (
                kit.sem(n) for n in ["squared", "summed", "rooted", "inverted", "scaled"])
            rows = GROUPS * TPB * HG
            PIECE = rows // TILES
            with nc.Block() as block:

                @block.vector
                def _(dve):
                    for i in range(TILES):
                        piece = o[:, i * PIECE * EB:(i + 1) * PIECE * EB]
                        if i > 0:
                            dve.wait_ge(summed, i)
                        dve.tensor_tensor(sq[:, :], piece, piece, ALU.mult).then_inc(squared, 1)
                        dve.wait_ge(squared, i + 1)
                        dve.tensor_reduce(ms[:, 0, i * PIECE:(i + 1) * PIECE],
                                          sq[:, :].rearrange("p (r e) -> p r e", e=EB), AX, ALU.add
                                          ).then_inc(summed, 1)
                    dve.wait_ge(rooted, 1)
                    dve.reciprocal(ms[:, 0, :], ms[:, 1, :]).then_inc(inverted, 1)
                    dve.wait_ge(inverted, 1)
                    all_o = o[:, :].rearrange("p (r e) -> p r e", e=EB)
                    dve.tensor_tensor(all_o, all_o, ms[:, 0, :].unsqueeze(2).to_broadcast([P, rows, EB]), ALU.mult
                                      ).then_inc(scaled, 1)
                    dve.wait_ge(scaled, 1)

                @block.scalar
                def _(act):
                    act.wait_ge(summed, TILES)
                    act.activation(ms[:, 1, :], ms[:, 0, :], ACT.Sqrt, bias=LN_EPS, scale=1.0 / EB
                                   ).then_inc(rooted, 1)

            project_out(nc, "b", o, EB, [wc[:, 0, :], wc[:, 1, :]], x, bank, ident)

        layernorm_transposed(nc, "ln3", x, xT, bank, ident)
        experts(nc, "f2", x, xT, d, bank, ident)

        stored = kit.sem("stored")
        with nc.Block() as block:

            @block.sync
            def _(sync):
                for b in range(B):
                    sync.dma_start(out[b].rearrange("(p t) d -> p t d", t=TPB),
                                   x[:, b * TPB:(b + 1) * TPB, :]).then_inc(stored, 16)
                sync.wait_ge(stored, 32)


def constants():
    inv = (1.0 / 10000.0 ** (np.arange(0, DH, 2, dtype=np.float32) / DH)).astype(np.float32)
    pos = (np.arange(P)[None, :] * TPB + np.arange(TPB)[:, None]).reshape(-1).astype(np.float32)
    theta = (pos[None, :] * inv[:, None]).astype(np.float32)
    row = (np.arange(P) % DH) // 2
    sign = np.where(np.arange(P) % 2 == 0, -1.0, 1.0).astype(np.float32)
    return {"cos": np.cos(theta).astype(np.float32)[row],
            "sin": (np.sin(theta).astype(np.float32)[row] * sign[:, None]).astype(np.float32),
            "ident": np.eye(P, dtype=np.float32)}


def kernel(**inputs):
    import concourse.bacc as bacc
    from concourse.bass_utils import run_bass_kernel_spmd

    g = {n: np.asarray(v) for n, v in inputs.items()}
    other = np.arange(P) ^ 1
    a, b, f = "L0_attn_a_", "L0_attn_b_", "L0_ffn_"
    arrays = {
        "x": g[a + "x"],
        "WqT": g[a + "Wq"].T, "WqT2": g[a + "Wq"][other].T, "WkT": g[a + "Wk"].T, "WkT2": g[a + "Wk"][other].T,
        "WvT": g[a + "Wv"].T, "WoT": g[a + "Wo"].T,
        "bq": g[a + "bq"], "bq2": g[a + "bq"][other], "bk": g[a + "bk"], "bk2": g[a + "bk"][other],
        "bv": g[a + "bv"], "bo": g[a + "bo"],
        "q1T": g[b + "q1_w"].T, "k1T": g[b + "k1_w"].T, "q2T": g[b + "q2_w"].T, "k2T": g[b + "k2_w"].T,
        "vT": g[b + "v_w"].T, "cT": g[b + "c_w"].T,
        "gamma": g[b + "bn_gamma"], "beta": g[b + "bn_beta"], "subln": np.tile(g[b + "subln_w"], P // (2 * DH)),
        "lq1": g[b + "lq1"], "lk1": g[b + "lk1"], "lq2": g[b + "lq2"], "lk2": g[b + "lk2"],
        "gate_w": g[f + "gate_w"], "w1": g[f + "w1"], "b1": g[f + "b1"].reshape(E, FC, P).transpose(2, 0, 1), "w2": g[f + "w2"], "b2": g[f + "b2"],
        **constants(),
    }
    nc = bacc.Bacc("TRN2", target_bir_lowering=False, num_devices=1)
    named, d = {}, {}
    for name, v in arrays.items():
        v = np.ascontiguousarray(v)
        named[f"in_{name}"] = v
        d[name] = nc.dram_tensor(f"in_{name}", v.shape, mybir.dt.from_np(v.dtype), kind="ExternalInput").ap()
    out = nc.dram_tensor("out_x", (B, N, D), F32, kind="ExternalOutput").ap()
    hybrid_kernel(nc, d, out)
    r = run_bass_kernel_spmd(nc, [named], core_ids=[0])
    return r.results[0]["out_x"]
```

```python
import math
from contextlib import ExitStack

import numpy as np
import concourse.bass as bass
from concourse import mybir

F32 = mybir.dt.float32
BF16 = mybir.dt.bfloat16
ACT = mybir.ActivationFunctionType
ALU = mybir.AluOpType
AX = mybir.AxisListType.X

P = 128
B, N, D = 2, 1024, 128
TOK = B * N
TPB = N // P
TILES = TOK // P
CH = 512
CHUNKS = TOK // CH
TPC = CH // P
H, DH = 16, 8
HG = 4
GPB = H // HG
GROUPS = B * GPB
VC = 32
E, FF = 8, 512
FC = FF // P
BLOCKS = TILES + E - 1
LN_EPS = 1e-5
LAMBDA_INIT = 0.8 - 0.6 * math.exp(-0.3)
SCALE = 1.0 / math.sqrt(DH)

PRODUCTS = [(0, 0), (0, 1), (0, 2), (1, 0), (1, 1), (2, 0)]
RUNS = [(0, 3), (3, 2), (5, 1)]
TWO_ONES = float(np.array([0x3F803F80], np.uint32).view(np.float32)[0])
HALF = 64
MAXROW = DH * len(PRODUCTS)


class Kit:

    def __init__(self, nc, life):
        self.nc, self.life, self.sems = nc, life, []

    def sb(self, name, shape, dtype=F32):
        return self.life.enter_context(self.nc.sbuf_tensor(name, shape, dtype))

    def sem(self, name):
        self.sems.append(self.nc.alloc_semaphore(name))
        return self.sems[-1]

    def release(self):
        self.nc.clear_and_free_semaphores(self.sems)
        self.nc.all_engine_barrier()


class LayerNorm:

    def __init__(self, k, tag, x, xT, xn, bank, ident):
        self.x, self.xT, self.xn, self.bank, self.ident = x, xT, xn, bank, ident
        self.stats = k.sb(f"stats_{tag}", [P, TILES, 6])
        self.mv = k.sb(f"mv_{tag}", [P, TILES, 2])
        self.std = k.sb(f"std_{tag}", [P, TILES])
        self.rstd = k.sb(f"rstd_{tag}", [P, TILES])
        self.stats_done, self.mv_done = k.sem(f"stats_done_{tag}"), k.sem(f"mv_done_{tag}")
        self.std_done, self.rstd_done = k.sem(f"std_done_{tag}"), k.sem(f"rstd_done_{tag}")
        self.xn_done, self.turned = k.sem(f"xn_done_{tag}"), k.sem(f"turned_{tag}")
        self.copied = k.sem(f"copied_{tag}")

    def vector(self, dve, ready):
        tiles = lambda c: range(c * TPC, (c + 1) * TPC)

        def statistics(c):
            ready(dve, c)
            for t in tiles(c):
                dve.bn_stats(self.stats[:, t, :], self.x[:, t, :]).then_inc(self.stats_done, 1)
            dve.wait_ge(self.stats_done, TPC * (c + 1))
            for t in tiles(c):
                dve.bn_aggr(self.mv[:, t, :], self.stats[:, t, :]).then_inc(self.mv_done, 1)

        def normalise(c):
            dve.wait_ge(self.std_done, c + 1)
            dve.reciprocal(self.rstd[:, c * TPC:(c + 1) * TPC], self.std[:, c * TPC:(c + 1) * TPC]
                           ).then_inc(self.rstd_done, 1)
            dve.wait_ge(self.rstd_done, c + 1)
            for t in tiles(c):
                dve.tensor_scalar(self.xn[:, t, :], self.x[:, t, :], self.mv[:, t, 0:1], self.rstd[:, t:t + 1],
                                  ALU.subtract, ALU.mult).then_inc(self.xn_done, 1)

        statistics(0)
        for c in range(CHUNKS):
            if c + 1 < CHUNKS:
                statistics(c + 1)
            normalise(c)

    def scalar(self, act):
        def root(c):
            act.wait_ge(self.mv_done, TPC * (c + 1))
            act.activation(self.std[:, c * TPC:(c + 1) * TPC], self.mv[:, c * TPC:(c + 1) * TPC, 1], ACT.Sqrt,
                           bias=LN_EPS).then_inc(self.std_done, 1)

        def copy(c):
            act.wait_ge(self.turned, c + 1)
            act.copy(self.xT[:, c * CH:(c + 1) * CH], self.bank[c % 2][:, :]).then_inc(self.copied, 1)

        root(0)
        for c in range(CHUNKS):
            if c + 1 < CHUNKS:
                root(c + 1)
            copy(c)

    def tensor(self, pe, use):
        for c in range(CHUNKS):
            pe.wait_ge(self.xn_done, TPC * (c + 1))
            if c >= 2:
                pe.wait_ge(self.copied, c - 1)
            for i in range(TPC):
                last = pe.transpose(self.bank[c % 2][:, i * P:(i + 1) * P], self.xn[:, c * TPC + i, :], self.ident)
            last.then_inc(self.turned, 1)
            if c > 0:
                pe.wait_ge(self.copied, c)
                use(c - 1)
        pe.wait_ge(self.copied, CHUNKS)
        use(CHUNKS - 1)


def attention(nc, tag, maps, qs, ks, vt, o, bank, ident, identb, e_dim, neg_lam, fill, beside=None,
              batch1_free=None):
    STEPS = TPB
    LEAD = 4
    QT = TPC
    LAST = (maps - 1, GROUPS - 1, 1)
    ALL = maps * GROUPS * 2

    def count(pos):
        m, g, half = pos
        return (m * GROUPS + g) * 2 + half

    def is_at(pos, where):
        return isinstance(pos[1], int) and pos == where

    def is_first(pos):
        return is_at(pos, (0, 0, 0))

    def after(pos):
        m, g, half = pos
        if is_at(pos, LAST):
            return None
        if half == 0:
            return (m, g, 1)
        return (m + 1, 0, 0) if isinstance(g, int) and g == GROUPS - 1 else (m, g + 1, 0)

    def bank_free(i):
        previous = i - 3 if i >= 3 else max(j for j in range(STEPS * HG) if j % 3 == i % 3) - STEPS * HG
        return previous + 1 - i

    def tiles_before(engine, pos, step):
        m, g, half = pos
        base = (m * GROUPS + g) * (2 * STEPS * HG)
        more = (half * STEPS + step) * HG
        if isinstance(g, int):
            return base + more
        with engine.register(f"tiles_{tag}_{nc.next_id()}") as tiles:
            engine.reg_add(tiles, base, more)
            return engine.snap(tiles)

    def everything(engine, half_group, filled=None):
        for m in range(maps):
            for half in range(2):
                half_group((m, 0, half))
            if filled is not None:
                if m == 0:
                    engine.wait_ge(filled[0, 0], fill.total)
                spans = [(1, GPB - 1), (GPB - 1, GROUPS - 1)]
            else:
                spans = [(1, GROUPS - 1)]
            for n, (start, end) in enumerate(spans):
                if n == 1:
                    engine.wait_ge(filled[m, 1], fill.total_again if m else fill.total)
                with engine.Fori(start, end) as g:
                    for half in range(2):
                        half_group((m, g, half))
            for half in range(2):
                half_group((m, GROUPS - 1, half))

    with ExitStack() as life:
        k = Kit(nc, life)
        vs = k.sb(f"vs_{tag}", [P, TPB, HG, VC])
        probs = k.sb(f"probs_{tag}", [P, 2, HG, CH])
        ots = k.sb(f"ots_{tag}", [P, CH])
        mx = k.sb(f"mx_{tag}", [P, 2, HG, QT, 2])
        nmax = k.sb(f"nmax_{tag}", [P, QT, HG])
        nmaxb = k.sb(f"nmaxb_{tag}", [P, QT, HG, 2], BF16)
        maxrows = k.sb(f"maxrows_{tag}", [HG * 2, CH], BF16)
        rec = k.sb(f"rec_{tag}", [P, QT, HG])
        tmp = k.sb(f"tmp_{tag}", [P, QT, HG, e_dim])
        names = ["max_scored", "max_taken", "max_joined", "max_split", "max_turned", "max_copied",
                 "max_rows", "scored", "exped", "multiplied", "v_ones", "v_staged", "o_copied",
                 "o_turned", "turn_read", "o_rec", "o_done"]
        s = {n: k.sem(f"{n}_{tag}") for n in names}
        filled = {(m, b): k.sem(f"filled{m}{b}_{tag}") for m in range(maps) for b in range(B)}
        score_bank, max_bank = bank[0:3], bank[3:6]
        out_bank, turn_bank = bank[6], bank[7]
        turnb = turn_bank[:, :].bitcast(BF16)

        def q_from(g, first):
            return g * (HG * N) + first

        def k_from(g, first):
            return g * (HG // 2 * N) + first

        def q_at(column, h, n):
            return qs[:, bass.ds(column + h * N, n)]

        def k_at(column, h, n):
            return ks[:, bass.ds(column + (h // 2) * N, n)]

        with nc.Block() as block:

            @block.tensor
            def _(pe):
                def max_scores(pos, step):
                    m, g, half = pos
                    if step == 0 and is_at(pos, (1, 0, 0)):
                        pe.wait_ge(filled[1, 0], fill.total_again)
                    tiles = tiles_before(pe, pos, step)
                    queries = q_from(g, half * CH + (step // 2) * P)
                    keys = k_from(g, (step % 2) * CH)

                    def one(h):
                        i = step * HG + h
                        if not (is_first(pos) and i < 3):
                            pe.wait_ge(s["max_taken"], tiles + h + bank_free(i))
                        pe.matmul(max_bank[i % 3][:, :], q_at(queries, h, P), k_at(keys, h, CH),
                                  start=True, stop=True).then_inc(s["max_scored"], 1)
                    return one

                def turn_max(pos):
                    pe.wait_ge(s["max_split"], 2 * (count(pos) + 1))
                    if not is_first(pos) and not is_at(pos, (0, 0, 1)):
                        pe.wait_ge(s["turn_read"], count(pos) - 1)
                    for j in range(QT):
                        last = pe.transpose(turnb[0:HG * 2, j * P:(j + 1) * P],
                                            nmaxb[:, j, :, :].rearrange("p h c -> p (h c)"), identb)
                    last.then_inc(s["max_turned"], 1)

                def scores(pos, step):
                    m, g, half = pos
                    tiles = tiles_before(pe, pos, step)
                    keys = k_from(g, step * P)
                    queries = q_from(g, half * CH)
                    if step == 0:
                        pe.wait_ge(s["max_rows"], 16 * HG * (count(pos) + 1))

                    def one(h):
                        i = step * HG + h
                        if not (is_first(pos) and i < 3):
                            pe.wait_ge(s["exped"], tiles + h + bank_free(i))
                        pe.matmul(score_bank[i % 3][:, :], k_at(keys, h, P), q_at(queries, h, CH),
                                  start=True, stop=True).then_inc(s["scored"], 1)
                    return one

                def multiply(pos, step):
                    m, g, half = pos
                    pe.wait_ge(s["exped"], HG * (count(pos) * STEPS + step + 1))
                    if half == 0 and step == 0:
                        pe.wait_ge(s["v_staged"], 2 * (m * GROUPS + g) + 1)
                    if half == 0 and step == TPB - 1:
                        pe.wait_ge(s["v_staged"], 2 * (m * GROUPS + g) + 2)
                    if step == 0 and not is_first(pos):
                        pe.wait_ge(s["o_copied"], count(pos))
                    for h in range(HG):
                        last = pe.matmul(out_bank[VC * h:VC * (h + 1), :], vs[:, step, h, :],
                                         probs[:, step % 2, h, :],
                                         start=(step == 0), stop=(step == STEPS - 1))
                    last.then_inc(s["multiplied"], 1)

                def turn_out(pos):
                    n = count(pos)
                    pe.wait_ge(s["o_copied"], n + 1)
                    if is_at(pos, LAST):
                        pe.wait_ge(s["turn_read"], n)
                    else:
                        pe.wait_ge(s["max_copied"], n + 2)
                    for i in range(QT):
                        last = pe.transpose(turn_bank[:, i * P:(i + 1) * P], ots[:, i * P:(i + 1) * P], ident)
                    last.then_inc(s["o_turned"], 1)

                before = None

                def half_group(pos):
                    nonlocal before
                    nxt = after(pos)
                    nxt2 = after(nxt) if nxt else None
                    if not is_first(pos):
                        m, g, half = pos
                        before = (m, g, 0) if half else ((m - 1, GROUPS - 1, 1) if isinstance(g, int) and g == 0
                                                         else (m, g - 1, 1))
                    for step in range(STEPS):
                        ahead, where = (step + LEAD, nxt) if step + LEAD < STEPS else (step + LEAD - STEPS, nxt2)
                        score = scores(pos, step)
                        max_score = max_scores(where, ahead) if where else None
                        for h in range(HG):
                            score(h)
                            if max_score:
                                max_score(h)
                        if step > 0:
                            multiply(pos, step - 1)
                        elif before:
                            multiply(before, STEPS - 1)
                        if step == 1 and before:
                            turn_out(before)
                        if step == STEPS - LEAD and nxt:
                            turn_max(nxt)

                for step in range(STEPS):
                    for h in range(HG):
                        max_scores((0, 0, 0), step)(h)
                for step in range(LEAD):
                    for h in range(HG):
                        max_scores((0, 0, 1), step)(h)
                    if step == 0:
                        turn_max((0, 0, 0))
                everything(pe, half_group, filled)
                multiply(LAST, STEPS - 1)
                turn_out(LAST)

            @block.scalar
            def _(act):
                def exponentials(pos, step):
                    tiles = tiles_before(act, pos, step)
                    for h in range(HG):
                        i = step * HG + h
                        act.wait_ge(s["scored"], tiles + h + 1)
                        if h == 0 and not (is_first(pos) and step < 2):
                            act.wait_ge(s["multiplied"], count(pos) * STEPS + step - 1)
                        act.activation(probs[:, step % 2, h, :], score_bank[i % 3][:, :], ACT.Exp, scale=SCALE
                                       ).then_inc(s["exped"], 1)

                def copy_out(n, first=False):
                    act.wait_ge(s["multiplied"], TPB * (n + 1))
                    if not first:
                        act.wait_ge(s["o_turned"], n)
                    act.copy(ots[:, :], out_bank[:, :]).then_inc(s["o_copied"], 1)

                def copy_max(n, first=False):
                    act.wait_ge(s["max_turned"], n + 1)
                    if not first:
                        act.wait_ge(s["max_rows"], 16 * HG * n)
                    act.copy(maxrows[:, :], turnb[0:HG * 2, 0:CH]).then_inc(s["max_copied"], 1)

                def half_group(pos):
                    n = count(pos)
                    for step in range(STEPS):
                        exponentials(pos, step)
                        if step == 0 and not is_first(pos):
                            copy_out(n - 1, first=is_at(pos, (0, 0, 1)))
                        if step == STEPS - LEAD + 1 and not is_at(pos, LAST):
                            copy_max(n + 1)

                copy_max(0, first=True)
                everything(act, half_group)
                copy_out(ALL - 1)

            @block.vector
            def _(dve):
                def take_max(pos, step, between=()):
                    tiles = tiles_before(dve, pos, step)
                    m, g, half = pos
                    for h in range(HG):
                        dve.wait_ge(s["max_scored"], tiles + h + 1)
                        dve.tensor_reduce(mx[:, half, h, step // 2, step % 2:step % 2 + 1],
                                          max_bank[(step * HG + h) % 3][:, :], AX, ALU.max
                                          ).then_inc(s["max_taken"], 1)
                        if h < len(between):
                            between[h]()

                def split_max(pos):
                    m, g, half = pos
                    n = count(pos)

                    def join():
                        dve.wait_ge(s["max_taken"], HG * STEPS * (n + 1))
                        dve.tensor_tensor(nmax[:, :, :].rearrange("p j h -> p h j"), mx[:, half, :, :, 0],
                                          mx[:, half, :, :, 1], ALU.max).then_inc(s["max_joined"], 1)

                    def high():
                        dve.wait_ge(s["max_joined"], n + 1)
                        if not is_first(pos):
                            dve.wait_ge(s["max_turned"], n)
                        dve.tensor_scalar(nmaxb[:, :, :, 0], nmax[:, :, :], -1.0, None, ALU.mult
                                          ).then_inc(s["max_split"], 1)

                    def low():
                        dve.wait_ge(s["max_split"], 2 * n + 1)
                        dve.scalar_tensor_tensor(out=nmaxb[:, :, :, 1], in0=nmax[:, :, :], scalar=-1.0,
                                                 in1=nmaxb[:, :, :, 0], op0=ALU.mult, op1=ALU.subtract
                                                 ).then_inc(s["max_split"], 1)

                    return [join, high, low]

                def divide(pos):
                    m, g, half = pos
                    n = count(pos)
                    t = turn_bank[:, :].rearrange("p (i h c) -> p i h c", i=QT, h=HG)
                    r = rec[:, :, :].unsqueeze(3).to_broadcast([P, QT, HG, e_dim])

                    def where():
                        tiles = o[:, :].rearrange("p (t w) -> p t w", t=TILES)
                        return tiles[:, bass.ds((g // GPB) * TPB + half * TPC, TPC),
                                     bass.ds((g % GPB) * HG * e_dim, HG * e_dim)]

                    def invert():
                        dve.wait_ge(s["o_turned"], n + 1)
                        dve.reciprocal(rec[:, :, :], t[:, :, :, e_dim]).then_inc(s["o_rec"], 1)

                    def quotients():
                        dve.wait_ge(s["o_rec"], n + 1)
                        out = where().rearrange("p i (h e) -> p i h e", h=HG) if m == 0 else tmp[:, :, :, :]
                        dve.tensor_tensor(out, t[:, :, :, 0:e_dim], r, ALU.mult).then_inc(s["turn_read"], 1)

                    def take_off():
                        dve.wait_ge(s["turn_read"], n + 1)
                        dve.scalar_tensor_tensor(out=where(), in0=tmp[:, :, :, :].rearrange("p i h e -> p i (h e)"),
                                                 scalar=neg_lam, in1=where(), op0=ALU.mult, op1=ALU.add
                                                 ).then_inc(s["o_done"], 1)

                    return [invert, quotients] + ([take_off] if m else [])

                def half_group(pos):
                    nxt = after(pos)
                    nxt2 = after(nxt) if nxt else None
                    m, g, half = pos
                    if half:
                        before = (m, g, 0)
                    elif isinstance(g, int) and g == 0:
                        before = (m - 1, GROUPS - 1, 1) if m else None
                    else:
                        before = (m, g - 1, 1)
                    for step in range(STEPS):
                        ahead, where = (step + LEAD, nxt) if step + LEAD < STEPS else (step + LEAD - STEPS, nxt2)
                        other = []
                        if step == STEPS - LEAD and nxt:
                            other = split_max(nxt)
                        if step == 2 and before:
                            other = divide(before)
                        if where:
                            take_max(where, ahead, other)
                        else:
                            for one in other:
                                one()

                for step in range(STEPS):
                    take_max((0, 0, 0), step)
                for step in range(LEAD):
                    take_max((0, 0, 1), step, split_max((0, 0, 0)) if step == 0 else ())
                everything(dve, half_group)
                for one in divide(LAST):
                    one()

            @block.gpsimd
            def _(pool):
                pool.memset(vs[:, :, :, :], 1.0).then_inc(s["v_ones"], 1)
                pool.wait_ge(s["v_ones"], 1)

                def stage(m, g):
                    n = m * GROUPS + g
                    v = vt[:, bass.ds(g * TPB * HG * e_dim, TPB * HG * e_dim)].rearrange(
                        "p (j h e) -> p j h e", j=TPB, h=HG)
                    first = m == 0 and isinstance(g, int) and g == 0
                    if not first:
                        pool.wait_ge(s["multiplied"], n * 2 * STEPS - 1)
                    pool.tensor_copy(vs[:, 0:TPB - 1, :, 0:e_dim], v[:, 0:TPB - 1]).then_inc(s["v_staged"], 1)
                    if not first:
                        pool.wait_ge(s["multiplied"], n * 2 * STEPS)
                    pool.tensor_copy(vs[:, TPB - 1, :, 0:e_dim], v[:, TPB - 1]).then_inc(s["v_staged"], 1)

                for m in range(maps):
                    stage(m, 0)
                    if m == 0 and beside:
                        beside(pool)
                    with pool.Fori(1, GROUPS) as g:
                        stage(m, g)

            @block.sync
            def _(sync):
                def write_max(pos):
                    m, g, half = pos
                    sync.wait_ge(s["max_copied"], count(pos) + 1)
                    for h in range(HG):
                        row = HALF * (h % 2) + MAXROW
                        sync.dma_start(qs[row:row + 2, bass.ds((g * HG + h) * N + half * CH, CH)],
                                       maxrows[2 * h:2 * h + 2, :]).then_inc(s["max_rows"], 16)

                def refill_batch(b):
                    sync.wait_ge(s["scored"], (b + 1) * GPB * 2 * STEPS * HG)
                    fill.start(sync, 1, b, filled[1, b], again=True)

                fill.start(sync, 0, 0, filled[0, 0], fill.SECOND)
                if batch1_free:
                    sync.wait_ge(*batch1_free)
                fill.start(sync, 0, 1, filled[0, 1])
                for m in range(maps):
                    for half in range(2):
                        write_max((m, 0, half))
                        if m == 1 and half == 0:
                            refill_batch(1)
                    with sync.Fori(1, GPB) as g:
                        for half in range(2):
                            write_max((m, g, half))
                    write_max((m, GPB, 0))
                    if maps == 2 and m == 0:
                        refill_batch(0)
                    write_max((m, GPB, 1))
                    with sync.Fori(GPB + 1, GROUPS) as g:
                        for half in range(2):
                            write_max((m, g, half))
                sync.wait_ge(s["max_rows"], 16 * HG * ALL)

        k.release()


def stack_side(sync, parts, side, b, pairs, qs, ks, done):
    j0, j1 = pairs
    for first, n in RUNS:
        for a in range(2):
            mine = parts[side, b, a]
            row = HALF * a + DH * first
            if side == 0:
                dst = qs[row:row + n * DH, b * H * N:(b + 1) * H * N].rearrange(
                    "p (j a t) -> p a j t", a=2, t=N)[:, a, j0:j1]
                src = mine[0:n, :, j0:j1].rearrange("i d j t -> (i d) j t")
            else:
                kp = PRODUCTS[first][0]
                dst = ks[row:row + n * DH, (b * H // 2 + j0) * N:(b * H // 2 + j1) * N]
                src = mine[kp:kp + 1, :, j0:j1].rearrange("i d j t -> i d (j t)").to_broadcast(
                    [n, DH, (j1 - j0) * N])
            sync.dma_start(dst, src).then_inc(done, 16)


def clear_maxima(sync, batches, qs, done):
    pairs = qs[:, batches[0] * H * N:(batches[-1] + 1) * H * N].rearrange("p (j a t) -> p a j t", a=2, t=N)
    for a in range(2):
        mine, zero = HALF * a + MAXROW, HALF * (1 - a) + MAXROW
        sync.dma_start(pairs[mine:mine + 2, a], pairs[zero:zero + 2, a]).then_inc(done, 16)


class Fill:

    ALL = (0, H // 2)
    FIRST, SECOND = (0, H // 4), (H // 4, H // 2)

    total = 16 * 2 * 2 * len(RUNS)
    total_again = total + 16 * 2

    def __init__(self, parts_dram, qs, ks):
        self.parts_dram, self.qs, self.ks = parts_dram, qs, ks

    def start(self, sync, m, b, done, pairs=ALL, again=False):
        if again:
            clear_maxima(sync, [b], self.qs, done)
        for side in range(2):
            stack_side(sync, self.parts_dram[m], side, b, pairs, self.qs, self.ks, done)


def prepare(nc, tag, xT, sides, v, fill, bank, rope=None, again=False,
            first_dma=None):
    UNITS = len(sides) * CHUNKS
    BUFS = 4
    PER = N // CH
    SETS = UNITS // PER
    SET_BUFS = 4
    with ExitStack() as life:
        k = Kit(nc, life)
        parts = k.sb(f"parts_{tag}", [P, SET_BUFS, 3, N], BF16)
        rest = k.sb(f"rest_{tag}", [P, BUFS, CH])
        x32 = k.sb(f"x32_{tag}", [P, BUFS, CH]) if rope else None
        t1 = k.sb(f"t1_{tag}", [P, 2, CH]) if rope else None
        t2 = k.sb(f"t2_{tag}", [P, 2, CH]) if rope else None
        names = ["projected", "rot1", "rot2", "rotated", "high", "minus_high", "mid", "low", "stacked", "zeroed",
                 "v_done", "v_taken"]
        s = {n: k.sem(f"{n}_{tag}") for n in names}
        parts_out = [k.sem(f"parts_out{j}_{tag}") for j in range(SET_BUFS)]

        def set_of(n):
            return n // (2 * B) * 2 + n % 2, n // 2 % B

        def unit(u):
            side, b = set_of(u // PER)
            return side, b * PER + u % PER

        def part(u, i):
            return parts[:, u // PER % SET_BUFS, i, (u % PER) * CH:(u % PER + 1) * CH]

        v_w, vt, v_bias, e_dim = v
        width = H * e_dim
        tiles_per_bank = CH // width
        V_UNITS = TILES // tiles_per_bank
        if rope:
            banks = lambda u: bank[2 * (u % 2):2 * (u % 2) + 2]
        else:
            banks = lambda u: bank[u % BUFS:u % BUFS + 1]

        with nc.Block() as block:

            @block.tensor
            def _(pe):
                def v_unit(u):
                    if u >= 2:
                        pe.wait_ge(s["v_taken"], u - 1)
                    for i in range(tiles_per_bank):
                        t = u * tiles_per_bank + i
                        last = pe.matmul(bank[4 + u % 2][:, i * width:(i + 1) * width], xT[:, t * P:(t + 1) * P],
                                         v_w, start=True, stop=True)
                    last.then_inc(s["v_done"], 1)

                for u in range(UNITS):
                    side, c = unit(u)
                    if rope and u >= 2:
                        pe.wait_ge(s["rot2"], u - 1)
                    if not rope and u >= BUFS:
                        pe.wait_ge(s["minus_high"], u - BUFS + 1)
                    for w, psum in zip(sides[side], banks(u)):
                        last = pe.matmul(psum[:, :], w, xT[:, c * CH:(c + 1) * CH], start=True, stop=True)
                    last.then_inc(s["projected"], 1)
                    if u >= UNITS - V_UNITS:
                        v_unit(u - (UNITS - V_UNITS))

            def v_places(u):
                t0 = u * tiles_per_bank
                b, j0 = t0 // TPB, t0 % TPB
                out = vt[:, b * GPB * TPB * HG * e_dim:(b + 1) * GPB * TPB * HG * e_dim].rearrange(
                    "p (g j c) -> p j g c", g=GPB, j=TPB)[:, j0:j0 + tiles_per_bank]
                return out, bank[4 + u % 2][:, :].rearrange("p (j g c) -> p j g c", j=tiles_per_bank, g=GPB)

            @block.vector
            def _(dve):
                def rotate(u):
                    side, c = unit(u)
                    cos, sin = rope
                    cols = slice((c % 2) * CH, (c % 2 + 1) * CH)
                    _, _, bias, bias_other = sides[side]
                    dve.wait_ge(s["projected"], u + 1)
                    if u >= 2:
                        dve.wait_ge(s["rotated"], u - 1)
                    dve.scalar_tensor_tensor(out=t1[:, u % 2, :], in0=banks(u)[0][:, :], scalar=bias,
                                             in1=cos[:, cols], op0=ALU.add, op1=ALU.mult).then_inc(s["rot1"], 1)
                    dve.scalar_tensor_tensor(out=t2[:, u % 2, :], in0=banks(u)[1][:, :], scalar=bias_other,
                                             in1=sin[:, cols], op0=ALU.add, op1=ALU.mult).then_inc(s["rot2"], 1)

                def subtract_high(u):
                    j = u % BUFS
                    dve.wait_ge(s["high"], u + 1)
                    if u >= BUFS:
                        dve.wait_ge(s["low"], u - BUFS + 1)
                    dve.tensor_tensor(rest[:, j, :], x32[:, j, :] if rope else banks(u)[0][:, :], part(u, 0),
                                      ALU.subtract).then_inc(s["minus_high"], 1)

                def low(u):
                    j = u % BUFS
                    dve.wait_ge(s["mid"], u + 1)
                    dve.tensor_tensor(part(u, 2), rest[:, j, :], part(u, 1), ALU.subtract
                                      ).then_inc(s["low"], 1)

                def add_v_bias(u):
                    dve.wait_ge(s["v_done"], u + 1)
                    out, got = v_places(u)
                    bias = v_bias.rearrange("p (g c) -> p g c", g=GPB).unsqueeze(1).to_broadcast(
                        [P, tiles_per_bank, GPB, HG * e_dim])
                    dve.tensor_tensor(out, got, bias, ALU.add).then_inc(s["v_taken"], 1)

                lag = 2 if rope else 0
                for u in range(UNITS + lag + 1):
                    if rope and u < UNITS:
                        rotate(u)
                    if 0 <= u - lag < UNITS:
                        subtract_high(u - lag)
                    if u - lag - 1 >= 0:
                        low(u - lag - 1)
                    if v_bias is not None and 0 <= u - (UNITS - V_UNITS) < V_UNITS:
                        add_v_bias(u - (UNITS - V_UNITS))

            @block.gpsimd
            def _(pool):
                if rope:
                    for u in range(UNITS):
                        pool.wait_ge(s["rot1"], u + 1)
                        pool.wait_ge(s["rot2"], u + 1)
                        if u >= BUFS:
                            pool.wait_ge(s["minus_high"], u - BUFS + 1)
                        pool.tensor_tensor(x32[:, u % BUFS, :], t1[:, u % 2, :], t2[:, u % 2, :], ALU.add
                                           ).then_inc(s["rotated"], 1)

            @block.scalar
            def _(act):
                for u in range(UNITS + 1):
                    if u < UNITS:
                        j = u % BUFS
                        act.wait_ge(s["rotated"] if rope else s["projected"], u + 1)
                        n = u // PER
                        if n >= SET_BUFS:
                            act.wait_ge(parts_out[n % SET_BUFS], 32 * (n // SET_BUFS))
                        act.copy(part(u, 0), x32[:, j, :] if rope else banks(u)[0][:, :]).then_inc(s["high"], 1)
                    if u > 0:
                        j = (u - 1) % BUFS
                        act.wait_ge(s["minus_high"], u)
                        act.copy(part(u - 1, 1), rest[:, j, :]).then_inc(s["mid"], 1)
                    if v_bias is None and 0 <= u - (UNITS - V_UNITS) < V_UNITS:
                        act.wait_ge(s["v_done"], u - (UNITS - V_UNITS) + 1)
                        out, got = v_places(u - (UNITS - V_UNITS))
                        act.copy(out, got).then_inc(s["v_taken"], 1)

            @block.sync
            def _(sync):
                if first_dma:
                    first_dma(sync)
                if again:
                    clear_maxima(sync, range(B), fill.qs, s["zeroed"])
                for n in range(SETS + 1):
                    if n < SETS:
                        side, b = set_of(n)
                        sync.wait_ge(s["low"], PER * (n + 1))
                        for a in range(2):
                            sync.dma_start(fill.parts_dram[side // 2][side % 2, b, a].rearrange(
                                "i d j t -> (d j) i t"), parts[HALF * a:HALF * (a + 1), n % SET_BUFS, :, :]
                                ).then_inc(parts_out[n % SET_BUFS], 16)
                    if n in (1, 2):
                        sync.wait_ge(parts_out[n - 1], 32)
                        stack_side(sync, fill.parts_dram[0], n - 1, 0, fill.FIRST, fill.qs, fill.ks, s["stacked"])
                for j in range(SET_BUFS):
                    sync.wait_ge(parts_out[j], 32 * len(range(j, SETS, SET_BUFS)))
                if again:
                    sync.wait_ge(s["zeroed"], 16 * 2)
                sync.wait_ge(s["stacked"], fill.total)

        k.release()


class ProjectOut:

    def __init__(self, k, tag, o, e_dim, w, x, oT, bank, ident, rms=False):
        self.parts = e_dim * H // P
        self.e_dim, self.w, self.x, self.bank, self.ident, self.rms = e_dim, w, x, bank, ident, rms
        self.o = o.rearrange("p (c w) -> p c w", c=CHUNKS)
        self.tiles = o.rearrange("p (t m c) -> p t m c", t=TILES, m=self.parts)
        self.oT = oT.rearrange("p (j m t) -> p j m t", j=2, m=self.parts)
        self.turned, self.copied = k.sem(f"o_turned2_{tag}"), k.sem(f"oT_copied_{tag}")
        self.projected, self.added = k.sem(f"o_projected_{tag}"), k.sem(f"o_added_{tag}")
        if rms:
            rows = TPC * H
            self.squares = k.sb(f"o_squares_{tag}", [P, 2, rows * e_dim])
            self.sums = k.sb(f"o_sums_{tag}", [P, CHUNKS, 3, rows])
            self.squared, self.summed, self.rooted, self.inverted, self.scaled = (
                k.sem(f"o_{n}_{tag}") for n in ["squared", "summed", "rooted", "inverted", "scaled"])

    def tensor(self, pe):
        def turn(c):
            if self.rms:
                pe.wait_ge(self.scaled, c + 1)
            if c >= 2:
                pe.wait_ge(self.copied, c - 1)
            for i in range(TPC):
                for m in range(self.parts):
                    last = pe.transpose(self.bank[(c % 2) * self.parts + m][:, i * P:(i + 1) * P],
                                        self.tiles[:, c * TPC + i, m, :], self.ident)
            last.then_inc(self.turned, 1)

        def project(c):
            pe.wait_ge(self.copied, c + 1)
            if c >= 2:
                pe.wait_ge(self.added, c - 1)
            for i in range(TPC):
                for m in range(self.parts):
                    last = pe.matmul(self.bank[4 + c % 2][:, i * P:(i + 1) * P],
                                     self.oT[:, c % 2, m, i * P:(i + 1) * P], self.w[m],
                                     start=(m == 0), stop=(m == self.parts - 1))
            last.then_inc(self.projected, 1)

        turn(0)
        for c in range(CHUNKS):
            if c + 1 < CHUNKS:
                turn(c + 1)
            project(c)

    def scalar(self, act):
        def square(c):
            if c >= 2:
                act.wait_ge(self.summed, c - 1)
            act.activation(self.squares[:, c % 2, :], self.o[:, c, :], ACT.Square).then_inc(self.squared, 1)

        def root(c):
            act.wait_ge(self.summed, c + 1)
            act.activation(self.sums[:, c, 1, :], self.sums[:, c, 0, :], ACT.Sqrt, bias=LN_EPS,
                           scale=1.0 / self.e_dim).then_inc(self.rooted, 1)

        if self.rms:
            square(0)
            for c in range(CHUNKS):
                if c + 1 < CHUNKS:
                    square(c + 1)
                root(c)
        for c in range(CHUNKS):
            act.wait_ge(self.turned, c + 1)
            if c >= 2:
                act.wait_ge(self.projected, c - 1)
            for m in range(self.parts):
                last = act.copy(self.oT[:, c % 2, m, :], self.bank[(c % 2) * self.parts + m][:, :])
            last.then_inc(self.copied, 1)

    def vector(self, dve):
        def total(c):
            dve.wait_ge(self.squared, c + 1)
            dve.tensor_reduce(self.sums[:, c, 0, :], self.squares[:, c % 2, :].rearrange(
                "p (r e) -> p r e", e=self.e_dim), AX, ALU.add).then_inc(self.summed, 1)

        def invert(c):
            dve.wait_ge(self.rooted, c + 1)
            dve.reciprocal(self.sums[:, c, 2, :], self.sums[:, c, 1, :]).then_inc(self.inverted, 1)

        if self.rms:
            total(0)
            for c in range(CHUNKS):
                if c + 1 < CHUNKS:
                    total(c + 1)
                invert(c)

    def add(self, dve, c):
        dve.wait_ge(self.projected, c + 1)
        xc = self.x[:, c * TPC:(c + 1) * TPC, :].rearrange("p t d -> p (t d)")
        dve.tensor_tensor(xc, self.bank[4 + c % 2][:, :], xc, ALU.add).then_inc(self.added, 1)
        dve.wait_ge(self.added, c + 1)

    def gpsimd(self, pool):
        if self.rms:
            for c in range(CHUNKS):
                pool.wait_ge(self.inverted, c + 1)
                piece = self.o[:, c, :].rearrange("p (r e) -> p r e", e=self.e_dim)
                pool.tensor_tensor(piece, piece, self.sums[:, c, 2, :].unsqueeze(2).to_broadcast(
                    [P, TPC * H, self.e_dim]), ALU.mult).then_inc(self.scaled, 1)


class Room:

    def __init__(self, free):
        self.free, self.used = free[:, :].bitcast(F32), 0

    def sb(self, name, shape):
        n, names = int(np.prod(shape[1:])), "abc"[:len(shape) - 1]
        piece = self.free[:, self.used:self.used + n]
        self.used += n
        return piece.rearrange(f"p ({' '.join(names)}) -> p {' '.join(names)}", **dict(zip(names, shape[1:])))


def experts(nc, tag, x, xT, xn, d, bank, ident, tables, sorted_dram, before, room=None, out=None, loads=None,
            after=None):
    earlier, number, upto = tables
    sorted_x, sorted_y = sorted_dram
    W2 = FF + FC
    COLS = W2 + FC * D
    PAD = TILES // 2
    LOADS = [range(i, min(i + TPC, BLOCKS)) for i in range(0, BLOCKS, TPC)]
    with ExitStack() as life:
        k = Kit(nc, life)
        room = room or k
        weights = room.sb(f"weights_{tag}", [P, E, COLS])
        mine = room.sb(f"mine_{tag}", [P, 2, COLS])
        b2 = k.sb(f"b2_{tag}", [E, D])
        gw = k.sb(f"gw_{tag}", [P, E])
        rows = room.sb(f"rows_{tag}", [P, BLOCKS, D])
        rowsT = room.sb(f"rowsT_{tag}", [P, BLOCKS * P])
        h = k.sb(f"h_{tag}", [P, 2, FC, P])
        logit = k.sb(f"logit_{tag}", [P, TILES, E])
        prob = k.sb(f"prob_{tag}", [P, TILES, E])
        first = k.sb(f"first_{tag}", [P, TILES, E])
        chosen = k.sb(f"chosen_{tag}", [P, TILES, E])
        gate = k.sb(f"gate_{tag}", [P, TILES, E])
        place = k.sb(f"place_{tag}", [P, TILES, E])
        top = k.sb(f"top_{tag}", [P, 5, TILES])
        slot = k.sb(f"slot_{tag}", [P, TILES], mybir.dt.uint32)
        run = k.sb(f"run_{tag}", [P, 2, PAD + TILES, E])
        per = k.sb(f"per_{tag}", [P, 3, E])
        compared = k.sb(f"compared_{tag}", [P, BLOCKS, E])
        owner = k.sb(f"owner_{tag}", [P, BLOCKS])
        owner_id = k.sb(f"owner_id_{tag}", [P, BLOCKS], mybir.dt.int32)
        ones = k.sb(f"ones_{tag}", [P, P])
        gateT, fetched = xT[0:E, :], xn
        names = ["gw_in", "b_in", "ones_set", "padded", "routed", "shifted", "r_exp", "r_step", "selected", "counted",
                 "placed", "owned", "gated", "g_turned", "g_copied", "b2_done", "x_init", "scattered",
                 "rows_turned", "rowsT_copied", "w1_fetched", "w2_fetched", "hidden", "gelu", "y_done", "y_copied",
                 "y_out", "x_done", "stored"]
        s = {n: k.sem(f"{n}_{tag}") for n in names}
        w_in = [k.sem(f"w_in{e}_{tag}") for e in range(E)]
        rows_in = [k.sem(f"rows_in{i}_{tag}") for i in range(len(LOADS))]
        y_in = [k.sem(f"y_in{c}_{tag}") for c in range(CHUNKS)]
        hidden_bank, y_bank = bank[0:2], bank[2:4]
        flat = weights[:, :, :].rearrange("p e c -> p (e c)")
        first_stage = before(k)
        norm = LayerNorm(k, tag, x, xT, xn, bank[0:2], ident)
        if after:
            last_stage = after(k)

        with nc.Block() as block:

            @block.sync
            def _(sync):
                sync.dma_start(gw[:, :], d["gate_w"]).then_inc(s["gw_in"], 16)
                sync.dma_start(b2[:, :], d["b2"]).then_inc(s["b_in"], 16)
                sync.dma_start(weights[:, :, FF:W2], d["b1"]).then_inc(s["b_in"], 16)
                for e in range(E):
                    sync.dma_start(weights[:, e, 0:FF], d["w1"][e]).then_inc(w_in[e], 16)
                    sync.dma_start(weights[:, e, W2:].rearrange("p (c d) -> p c d", c=FC),
                                   d["w2"][e].rearrange("(c p) d -> p c d", p=P)).then_inc(w_in[e], 16)
                if loads:
                    loads(sync)
                sync.wait_ge(s["scattered"], 16 * TILES)
                for i, blocks in enumerate(LOADS):
                    sync.dma_start(rows[:, blocks.start:blocks.stop, :],
                                   sorted_x[blocks.start * P:blocks.stop * P, :].rearrange("(k p) d -> p k d", p=P)
                                   ).then_inc(rows_in[i], 16)

                def store(first_block, n):
                    sync.wait_ge(s["y_copied"], first_block + n)
                    sync.dma_start(sorted_y[bass.ds(first_block * P, n * P), :].rearrange("(k p) d -> p k d", p=P),
                                   rows[:, bass.ds(first_block, n), :]).then_inc(s["y_out"], 16)

                with sync.Fori(0, BLOCKS // 2) as pair:
                    store(pair * 2, 2)
                store(BLOCKS - 1, 1)
                sync.wait_ge(s["y_out"], 16 * (BLOCKS // 2 + 1))
                if out is not None:
                    for c in range(CHUNKS):
                        b, j = divmod(c * TPC, TPB)
                        sync.wait_ge(s["x_done"], TPC * (c + 1))
                        sync.dma_start(out[b].rearrange("(p t) d -> p t d", t=TPB)[:, j:j + TPC, :],
                                       x[:, c * TPC:(c + 1) * TPC, :]).then_inc(s["stored"], 16)
                    sync.wait_ge(s["stored"], 16 * CHUNKS)

            @block.gpsimd
            def _(pool):
                first_stage.gpsimd(pool)
                pool.memset(ones[:, :], 1.0).then_inc(s["ones_set"], 1)
                pool.memset(run[:, :, 0:PAD, :], 0.0).then_inc(s["padded"], 1)
                pool.wait_ge(s["placed"], 1)
                for t in range(TILES):
                    pool.indirect_dma_start(sorted_x[:, :], bass.IndirectOffsetOnAxis(ap=slot[:, t:t + 1], axis=0),
                                            xn[:, t, :], None).then_inc(s["scattered"], 16)
                pool.wait_ge(s["scattered"], 16 * TILES)

                pool.wait_ge(s["owned"], 1)
                for e in range(E):
                    pool.wait_ge(w_in[e], 32)

                def fetch(b, parity, first=False):
                    e = pool.value_load(owner_id[0:1, bass.ds(b, 1)], min_val=0, max_val=E - 1)
                    if not first:
                        pool.wait_ge(s["y_done"], b - 1)
                    pool.tensor_copy(mine[:, parity, W2:], flat[:, bass.ds(e * COLS + W2, FC * D)]
                                     ).then_inc(s["w2_fetched"], 1)

                fetch(0, 0, first=True)
                fetch(1, 1, first=True)
                with pool.Fori(1, BLOCKS // 2) as pair:
                    fetch(pair * 2, 0)
                    fetch(pair * 2 + 1, 1)
                fetch(BLOCKS - 1, 0)

                pool.wait_ge(s["y_out"], 16 * (BLOCKS // 2 + 1))
                for t in range(TILES):
                    pool.indirect_dma_start(fetched[:, t, :], None, sorted_y[:, :],
                                            bass.IndirectOffsetOnAxis(ap=slot[:, t:t + 1], axis=0)
                                            ).then_inc(y_in[t // TPC], 16)

            @block.tensor
            def _(pe):
                def route(c):
                    pe.wait_ge(s["gw_in"], 16)
                    for t in range(c * TPC, (c + 1) * TPC):
                        last = pe.matmul(bank[6][:, t * E:(t + 1) * E], xT[:, t * P:(t + 1) * P], gw[:, :],
                                         start=True, stop=True)
                    last.then_inc(s["routed"], 1)

                first_stage.tensor(pe)
                norm.tensor(pe, route)
                pe.wait_ge(s["ones_set"], 1)
                pe.wait_ge(s["selected"], 1)
                sel = chosen[:, :, :].rearrange("p t e -> p (t e)")
                pe.matmul(bank[7][:, 0:TILES * E], ones[:, :], sel, start=True, stop=True
                          ).then_inc(s["counted"], 1)
                pe.matmul(bank[5][:, 0:TILES * E], earlier, sel, start=True, stop=True).then_inc(s["counted"], 1)

                pe.wait_ge(s["b_in"], 32)
                pe.wait_ge(s["gated"], 1)
                for c in range(CHUNKS):
                    for i in range(TPC):
                        last = pe.transpose(bank[4 + c][0:E, i * P:(i + 1) * P], gate[:, c * TPC + i, :], ident)
                    last.then_inc(s["g_turned"], 1)
                for c in range(CHUNKS):
                    pe.wait_ge(s["g_copied"], c + 1)
                    for i in range(TPC):
                        t = c * TPC + i
                        last = pe.matmul(bank[c][:, i * P:(i + 1) * P], gateT[:, t * P:(t + 1) * P], b2[:, :],
                                         start=True, stop=True)
                    last.then_inc(s["b2_done"], 1)

                for i, blocks in enumerate(LOADS):
                    pe.wait_ge(rows_in[i], 16)
                    if i >= 2:
                        pe.wait_ge(s["rowsT_copied"], i - 1)
                    for j, b in enumerate(blocks):
                        last = pe.transpose(bank[4 + i % 2][:, j * P:(j + 1) * P], rows[:, b, :], ident)
                    last.then_inc(s["rows_turned"], 1)
                pe.wait_ge(s["x_init"], CHUNKS)
                pe.wait_ge(s["rowsT_copied"], len(LOADS))

                def hidden(b, parity, first=False):
                    pe.wait_ge(s["w1_fetched"], b + 1)
                    if not first:
                        pe.wait_ge(s["gelu"], b - 1)
                    for f in range(FC):
                        last = pe.matmul(hidden_bank[parity][:, f * P:(f + 1) * P],
                                         mine[:, parity, f * P:(f + 1) * P], rowsT[:, bass.ds(b * P, P)],
                                         start=True, stop=True)
                    last.then_inc(s["hidden"], 1)

                def down(b, parity, first=False):
                    pe.wait_ge(s["w2_fetched"], b + 1)
                    pe.wait_ge(s["gelu"], b + 1)
                    if not first:
                        pe.wait_ge(s["y_copied"], b - 1)
                    for f in range(FC):
                        last = pe.matmul(y_bank[parity][:, 0:D], h[:, parity, f, :],
                                         mine[:, parity, W2 + f * D:W2 + (f + 1) * D],
                                         start=(f == 0), stop=(f == FC - 1))
                    last.then_inc(s["y_done"], 1)

                hidden(0, 0, first=True)
                hidden(1, 1, first=True)
                down(0, 0, first=True)
                hidden(2, 0)
                down(1, 1, first=True)
                with pe.Fori(1, BLOCKS // 2) as pair:
                    b = pair * 2
                    hidden(b + 1, 1)
                    down(b, 0)
                    hidden(b + 2, 0)
                    down(b + 1, 1)
                down(BLOCKS - 1, 0)
                if after:
                    last_stage.tensor(pe)

            @block.scalar
            def _(act):
                first_stage.scalar(act)
                norm.scalar(act)
                act.wait_ge(s["shifted"], 1)
                act.activation(prob[:, :, :], logit[:, :, :], ACT.Exp).then_inc(s["r_exp"], 1)
                for i, blocks in enumerate(LOADS):
                    act.wait_ge(s["rows_turned"], i + 1)
                    n = len(blocks) * P
                    act.copy(rowsT[:, blocks.start * P:blocks.start * P + n], bank[4 + i % 2][:, 0:n]
                             ).then_inc(s["rowsT_copied"], 1)

                def gelu(b, parity, first=False):
                    act.wait_ge(s["hidden"], b + 1)
                    if not first:
                        act.wait_ge(s["y_done"], b - 1)
                    for f in range(FC):
                        last = act.activation(h[:, parity, f, :], hidden_bank[parity][:, f * P:(f + 1) * P],
                                              ACT.Gelu, bias=mine[:, parity, FF + f:FF + f + 1])
                    last.then_inc(s["gelu"], 1)

                def take(b, parity):
                    act.wait_ge(s["y_done"], b + 1)
                    act.copy(rows[:, bass.ds(b, 1), :].rearrange("p k d -> p (k d)"), y_bank[parity][:, 0:D]
                             ).then_inc(s["y_copied"], 1)

                gelu(0, 0, first=True)
                gelu(1, 1, first=True)
                take(0, 0)
                gelu(2, 0)
                take(1, 1)
                with act.Fori(1, BLOCKS // 2) as pair:
                    b = pair * 2
                    gelu(b + 1, 1)
                    take(b, 0)
                    gelu(b + 2, 0)
                    take(b + 1, 1)
                take(BLOCKS - 1, 0)
                if after:
                    last_stage.scalar(act)

            @block.vector
            def _(dve):
                shape = [P, TILES, E]
                over = lambda i: top[:, i, :].unsqueeze(2).to_broadcast(shape)
                by_expert = lambda ap, n: ap.unsqueeze(1).to_broadcast([P, n, E])
                steps = 0

                def done(ins):
                    nonlocal steps
                    steps += 1
                    ins.then_inc(s["r_step"], 1)
                    dve.wait_ge(s["r_step"], steps)

                first_stage.vector(dve)
                norm.vector(dve, first_stage.add)
                dve.wait_ge(s["routed"], CHUNKS)
                got = bank[6][:, 0:TILES * E].rearrange("p (t e) -> p t e", e=E)
                done(dve.tensor_reduce(top[:, 0, :], got, AX, ALU.max))
                dve.tensor_tensor(logit[:, :, :], got, over(0), ALU.subtract).then_inc(s["shifted"], 1)
                dve.wait_ge(s["r_exp"], 1)
                done(dve.tensor_reduce(top[:, 1, :], prob[:, :, :], AX, ALU.add))
                done(dve.reciprocal(top[:, 2, :], top[:, 1, :]))
                done(dve.tensor_tensor(prob[:, :, :], prob[:, :, :], over(2), ALU.mult))
                done(dve.tensor_reduce(top[:, 3, :], prob[:, :, :], AX, ALU.max))
                done(dve.tensor_tensor(first[:, :, :], prob[:, :, :], over(3), ALU.is_equal))
                done(dve.scalar_tensor_tensor(out=first[:, :, :], in0=by_expert(number[:, 0:E], TILES),
                                              scalar=-float(P), in1=first[:, :, :], op0=ALU.add, op1=ALU.mult))
                done(dve.tensor_reduce(top[:, 4, :], first[:, :, :], AX, ALU.min))
                dve.tensor_tensor(chosen[:, :, :], first[:, :, :], over(4), ALU.is_equal).then_inc(s["selected"], 1)

                dve.wait_ge(s["padded"], 1)
                dve.wait_ge(s["counted"], 1)
                whole = bank[7][:, 0:TILES * E].rearrange("p (t e) -> p t e", e=E)
                done(dve.tensor_copy(run[:, 0, PAD:, :], whole))
                for n, distance in enumerate([1, 2, 4, 8]):
                    done(dve.tensor_tensor(run[:, (n + 1) % 2, PAD:, :], run[:, n % 2, PAD:, :],
                                           run[:, n % 2, PAD - distance:PAD + TILES - distance, :], ALU.add))
                count = run[:, 0, PAD + TILES - 1, :]
                done(dve.scalar_tensor_tensor(out=compared[:, 0:TILES, :], in0=by_expert(count, TILES),
                                              scalar=1.0 / P, op0=ALU.mult, op1=ALU.is_gt,
                                              in1=number[:, 0:TILES].unsqueeze(2).to_broadcast(shape)))
                done(dve.tensor_reduce(per[:, 0, :], compared[:, 0:TILES, :].rearrange("p t e -> p e t"), AX, ALU.add))
                done(dve.tensor_tensor(compared[:, 0:E, :], by_expert(per[:, 0, :], E), upto, ALU.mult))
                done(dve.tensor_reduce(per[:, 1, :], compared[:, 0:E, :], AX, ALU.add))
                done(dve.tensor_tensor(per[:, 2, :], per[:, 1, :], per[:, 0, :], ALU.subtract))
                done(dve.scalar_tensor_tensor(out=place[:, :, :], in0=by_expert(per[:, 2, :], TILES),
                                              scalar=float(P), in1=run[:, 0, PAD - 1:PAD + TILES - 1, :],
                                              op0=ALU.mult, op1=ALU.add))
                dve.wait_ge(s["counted"], 2)
                done(dve.tensor_tensor(place[:, :, :], place[:, :, :],
                                       bank[5][:, 0:TILES * E].rearrange("p (t e) -> p t e", e=E), ALU.add))
                done(dve.tensor_tensor(place[:, :, :], place[:, :, :], chosen[:, :, :], ALU.mult))
                done(dve.tensor_reduce(top[:, 4, :], place[:, :, :], AX, ALU.add))
                dve.tensor_copy(slot[:, :], top[:, 4, :]).then_inc(s["placed"], 1)
                dve.tensor_tensor(gate[:, :, :], chosen[:, :, :], over(3), ALU.mult).then_inc(s["gated"], 1)
                done(dve.tensor_tensor(compared[:, :, :], by_expert(per[:, 1, :], BLOCKS),
                                       number[:, 0:BLOCKS].unsqueeze(2).to_broadcast([P, BLOCKS, E]), ALU.is_le))
                done(dve.tensor_reduce(owner[:, :], compared[:, :, :], AX, ALU.add))
                dve.tensor_scalar(owner_id[:, :], owner[:, :], float(E - 1), None, ALU.min).then_inc(s["owned"], 1)

                for c in range(CHUNKS):
                    dve.wait_ge(s["g_turned"], c + 1)
                    dve.tensor_copy(gateT[:, c * CH:(c + 1) * CH], bank[4 + c][0:E, :]).then_inc(s["g_copied"], 1)
                for c in range(CHUNKS):
                    dve.wait_ge(s["b2_done"], c + 1)
                    xc = x[:, c * TPC:(c + 1) * TPC, :].rearrange("p t d -> p (t d)")
                    dve.tensor_tensor(xc, bank[c][:, :], xc, ALU.add).then_inc(s["x_init"], 1)

                dve.wait_ge(s["owned"], 1)
                dve.wait_ge(s["b_in"], 32)
                for e in range(E):
                    dve.wait_ge(w_in[e], 32)

                def fetch(b, parity, first=False):
                    e = dve.value_load(owner_id[0:1, bass.ds(b, 1)], min_val=0, max_val=E - 1)
                    if not first:
                        dve.wait_ge(s["hidden"], b - 1)
                        dve.wait_ge(s["gelu"], b - 1)
                    dve.tensor_copy(mine[:, parity, 0:W2], flat[:, bass.ds(e * COLS, W2)]).then_inc(s["w1_fetched"], 1)

                fetch(0, 0, first=True)
                fetch(1, 1, first=True)
                with dve.Fori(1, BLOCKS // 2) as pair:
                    fetch(pair * 2, 0)
                    fetch(pair * 2 + 1, 1)
                fetch(BLOCKS - 1, 0)

                dve.wait_ge(s["x_init"], CHUNKS)

                def combine(dve, c):
                    dve.wait_ge(y_in[c], 16 * TPC)
                    for t in range(c * TPC, (c + 1) * TPC):
                        dve.scalar_tensor_tensor(out=x[:, t, :], in0=fetched[:, t, :], scalar=top[:, 3, t:t + 1],
                                                 in1=x[:, t, :], op0=ALU.mult, op1=ALU.add).then_inc(s["x_done"], 1)
                    if after:
                        dve.wait_ge(s["x_done"], TPC * (c + 1))

                if after:
                    last_stage.vector(dve, combine)
                else:
                    for c in range(CHUNKS):
                        combine(dve, c)
                dve.wait_ge(s["x_done"], TILES)

        k.release()


class BatchNorm:

    def __init__(self, k, x, xT, xn, bank, ident, gamma, beta, loaded, weights, weights_exp):
        self.xT, self.gamma, self.beta, self.loaded = xT, gamma, beta, loaded
        self.weights, self.weights_exp = weights, weights_exp
        self.stats = k.sb("bn_stats", [P, CHUNKS, 6])
        self.mv = k.sb("bn_mv", [P, 2])
        self.sc = k.sb("bn_sc", [P, 4])
        self.chain, self.std_done = k.sem("bn_chain"), k.sem("bn_std_done")
        self.norm = LayerNorm(k, "ln2", x, xT, xn, bank[0:2], ident)

    def vector(self, dve, ready):
        xT, stats, mv, sc, chain = self.xT, self.stats, self.mv, self.sc, self.chain
        self.norm.vector(dve, ready)
        self.weights(dve)
        dve.wait_ge(*self.loaded)
        for c in range(CHUNKS):
            dve.wait_ge(self.norm.copied, c + 1)
            dve.bn_stats(stats[:, c, :], xT[:, c * CH:(c + 1) * CH]).then_inc(chain, 1)
        dve.wait_ge(chain, CHUNKS)
        dve.bn_aggr(mv[:, :], stats[:, :, :].rearrange("p c s -> p (c s)")).then_inc(chain, 1)
        dve.wait_ge(self.std_done, 1)
        dve.reciprocal(sc[:, 1:2], sc[:, 0:1]).then_inc(chain, 1)
        dve.wait_ge(chain, CHUNKS + 2)
        dve.tensor_tensor(sc[:, 2:3], sc[:, 1:2], self.gamma, ALU.mult).then_inc(chain, 1)
        dve.wait_ge(chain, CHUNKS + 3)
        dve.tensor_scalar(sc[:, 3:4], mv[:, 0:1], sc[:, 2:3], -1.0, ALU.mult, ALU.mult).then_inc(chain, 1)
        dve.wait_ge(chain, CHUNKS + 4)
        dve.tensor_tensor(sc[:, 3:4], sc[:, 3:4], self.beta, ALU.add).then_inc(chain, 1)
        dve.wait_ge(chain, CHUNKS + 5)
        for c in range(CHUNKS):
            dve.tensor_scalar(xT[:, c * CH:(c + 1) * CH], xT[:, c * CH:(c + 1) * CH], sc[:, 2:3], sc[:, 3:4],
                              ALU.mult, ALU.add).then_inc(chain, 1)
        dve.wait_ge(chain, 2 * CHUNKS + 5)

    def scalar(self, act):
        self.norm.scalar(act)
        act.wait_ge(self.chain, CHUNKS + 1)
        act.activation(self.sc[:, 0:1], self.mv[:, 1:2], ACT.Sqrt, bias=LN_EPS).then_inc(self.std_done, 1)
        self.weights_exp(act)

    def tensor(self, pe):
        self.norm.tensor(pe, lambda c: None)


def hybrid_kernel(nc, d, out):
    with ExitStack() as life:
        kit = Kit(nc, life)
        bank = [life.enter_context(nc.psum_tensor(f"bank{i}", [P, CH], F32)) for i in range(8)]
        x = kit.sb("x", [P, TILES, D])
        xT = kit.sb("xT", [P, TOK])
        xn = kit.sb("xn", [P, TILES, D])
        qs = kit.sb("query_stacks", [P, B * H * N], BF16)
        ks = kit.sb("key_stacks", [P, B * H // 2 * N], BF16)
        identt = kit.sb("ident", [P, P])
        identbt = kit.sb("identb", [P, P], BF16)
        ident, identb = identt[:, :], identbt[:, :]
        earliert, numbert, uptot = kit.sb("earlier", [P, P]), kit.sb("number", [P, 24]), kit.sb("upto", [P, E, E])
        tables = (earliert[:, :], numbert[:, :], uptot[:, :, :])
        sorted_x = nc.dram_tensor("sorted_x", [BLOCKS * P, D], F32, kind="Internal").ap()
        sorted_y = nc.dram_tensor("sorted_y", [BLOCKS * P, D], F32, kind="Internal").ap()
        parts_dram = nc.dram_tensor("parts_dram", [2, 2, B, 2, 3, DH, H // 2, N], BF16, kind="Internal").ap()

        fill = Fill(parts_dram, qs, ks)

        x_in = [kit.sem(f"x_in{b}") for b in range(B)]
        norm = LayerNorm(kit, "ln0", x, xT, xn, bank[0:2], ident)
        cleared, ones_set, identb_set, ident_in, tables_in, slots_zero = (
            kit.sem(n) for n in ["cleared", "ones_set", "identb_set", "ident_in", "tables_in", "slots_zero"])

        wo = kit.sb("wo", [P, D])
        o = xn[:, :, :].rearrange("p t d -> p (t d)")
        with ExitStack() as phase:
            k = Kit(nc, phase)
            cos, sin = k.sb("cos", [P, N]), k.sb("sin", [P, N])
            wa = k.sb("wa", [P, 5, D])
            ba = k.sb("ba", [P, 4])
            bvo = k.sb("bvo", [P, 2, D])
            vt = k.sb("vt_a", [P, GROUPS * TPB * HG * DH])
            a_in, o_biased = kit.sem("a_in"), kit.sem("o_biased")

            with nc.Block() as block:

                @block.sync
                def _(sync):
                    for b in range(B):
                        sync.dma_start(x[:, b * TPB:(b + 1) * TPB, :],
                                       d["x"][b].rearrange("(p t) d -> p t d", t=TPB)).then_inc(x_in[b], 16)
                    sync.dma_start(ident, d["ident"]).then_inc(ident_in, 16)
                    sync.dma_start(earliert[:, :], d["earlier"]).then_inc(tables_in, 16)
                    sync.dma_start(numbert[:, :], d["number"].partition_broadcast(P)).then_inc(tables_in, 16)
                    sync.dma_start(uptot[:, :, :].rearrange("p e o -> p (e o)"), d["upto"].partition_broadcast(P)
                                   ).then_inc(tables_in, 16)
                    for i, w in enumerate(["WqT", "WqT2", "WkT", "WkT2", "WvT"]):
                        sync.dma_start(wa[:, i, :], d[w]).then_inc(a_in, 16)
                    for i, w in enumerate(["bq", "bq2", "bk", "bk2"]):
                        sync.dma_start(ba[:, i:i + 1], d[w].unsqueeze(1)).then_inc(a_in, 16)
                    sync.dma_start(cos[:, :], d["cos"]).then_inc(a_in, 16)
                    sync.dma_start(sin[:, :], d["sin"]).then_inc(a_in, 16)
                    sync.dma_start(wo[:, :], d["WoT"]).then_inc(a_in, 16)
                    for i, w in enumerate(["bv", "bo"]):
                        sync.dma_start(bvo[:, i, :], d[w].partition_broadcast(P)).then_inc(a_in, 16)
                    sync.wait_ge(cleared, 1)
                    sync.dma_start(sorted_x.rearrange("(p k) d -> p (k d)", p=P),
                                   qs[:, 0:2 * BLOCKS * D].bitcast(F32)).then_inc(slots_zero, 16)
                    sync.wait_ge(tables_in, 48)
                    sync.wait_ge(slots_zero, 16)
                    sync.wait_ge(a_in, 16 * 14)

                @block.gpsimd
                def _(pool):
                    pool.memset(qs[:, 0:H * N].bitcast(F32), 0.0).then_inc(cleared, 1)
                    pool.wait_ge(cleared, 1)
                    pool.memset(ks[HALF // 2:HALF, :].bitcast(F32), TWO_ONES).then_inc(ones_set, 1)

                @block.vector
                def _(dve):
                    norm.vector(dve, lambda dve, c: dve.wait_ge(x_in[c * B // CHUNKS], 16))
                    dve.wait_ge(ident_in, 16)
                    dve.tensor_copy(identb, ident).then_inc(identb_set, 1)

                @block.scalar
                def _(act):
                    norm.scalar(act)

                @block.tensor
                def _(pe):
                    pe.wait_ge(ident_in, 16)
                    norm.tensor(pe, lambda c: None)

            def other_ones(sync):
                sync.dma_start(ks[HALF + MAXROW:P, :], ks[MAXROW:HALF, :]).then_inc(ones_set, 16)
                sync.wait_ge(ones_set, 17)

            prepare(nc, "a", xT, [[wa[:, 0, :], wa[:, 1, :], ba[:, 0:1], ba[:, 1:2]],
                                  [wa[:, 2, :], wa[:, 3, :], ba[:, 2:3], ba[:, 3:4]]],
                    (wa[:, 4, :], vt, bvo[:, 0, :], DH), fill, bank, rope=(cos, sin),
                    first_dma=other_ones)

            def clear_and_add_bias(pool):
                pool.memset(qs[:, H * N:].bitcast(F32), 0.0).then_inc(cleared, 1)
                pool.tensor_tensor(x[:, :, :], x[:, :, :], bvo[:, 1, :].unsqueeze(1).to_broadcast([P, TILES, D]),
                                   ALU.add).then_inc(o_biased, 1)

            attention(nc, "a", 1, qs, ks, vt, o, bank, ident, identb, DH, None, fill, beside=clear_and_add_bias,
                      batch1_free=(cleared, 2))

        EB = 2 * DH
        wb = kit.sb("wb", [P, 4, D])
        wv = kit.sb("wv", [P, 2 * D])
        wc = kit.sb("wc", [P, 2, D])
        cols = kit.sb("cols", [P, 3])
        lams = kit.sb("lams", [P, 4, DH])
        lamp = kit.sb("lamp", [P, 2, DH])
        lamv = kit.sb("lamv", [P, 6])
        b_in, wb_in, lam_chain, lam_exp, wc_done = (
            kit.sem(n) for n in ["b_in", "wb_in", "lam_chain", "lam_exp", "wc_done"])

        def loads(sync):
            for i, w in enumerate(["lq1", "lk1", "lq2", "lk2"]):
                sync.dma_start(lams[:, i, :], d[w].partition_broadcast(P)).then_inc(b_in, 16)
            for i, w in enumerate(["gamma", "beta", "subln"]):
                sync.dma_start(cols[:, i:i + 1], d[w].unsqueeze(1)).then_inc(b_in, 16)
            sync.dma_start(wc[:, :, :], d["cT"].rearrange("(m p) n -> p m n", p=P)).then_inc(b_in, 16)
            for i, w in enumerate(["q1T", "k1T", "q2T", "k2T"]):
                sync.dma_start(wb[:, i, :], d[w]).then_inc(wb_in, 16)
            sync.dma_start(wv[:, :], d["vT"]).then_inc(wb_in, 16)
            sync.wait_ge(wb_in, 16 * 5)

        def weights(dve):
            dve.wait_ge(b_in, 16 * 8)
            for i in range(2):
                dve.tensor_tensor(lamp[:, i, :], lams[:, 2 * i, :], lams[:, 2 * i + 1, :], ALU.mult
                                  ).then_inc(lam_chain, 1)
            dve.wait_ge(lam_chain, 2)
            dve.tensor_reduce(lamv[:, 0:2], lamp[:, :, :], AX, ALU.add).then_inc(lam_chain, 1)
            dve.tensor_scalar(wc[:, :, :], wc[:, :, :], cols[:, 2:3], 1.0 - LAMBDA_INIT, ALU.mult, ALU.mult
                              ).then_inc(wc_done, 1)

        def weights_exp(act):
            act.wait_ge(lam_chain, 3)
            act.activation(lamv[:, 2:4], lamv[:, 0:2], ACT.Exp).then_inc(lam_exp, 1)

        def minus_lambda(pool):
            pool.tensor_tensor(lamv[:, 4:5], lamv[:, 3:4], lamv[:, 2:3], ALU.subtract).then_inc(lam_chain, 1)
            pool.wait_ge(lam_chain, 4)
            pool.tensor_scalar(lamv[:, 5:6], lamv[:, 4:5], -LAMBDA_INIT, None, ALU.add).then_inc(lam_chain, 1)
            pool.wait_ge(lam_chain, 5)

        experts(nc, "f1", x, xT, xn, d, bank, ident, tables, (sorted_x, sorted_y),
                before=lambda k: ProjectOut(k, "a", o, DH, [wo[:, :]], x, xT[:, 2 * CH:4 * CH], bank, ident),
                loads=loads,
                after=lambda k: BatchNorm(k, x, xT, xn, bank, ident, cols[:, 0:1], cols[:, 1:2],
                                                   (b_in, 16 * 8), weights, weights_exp))

        with ExitStack() as phase:
            k = Kit(nc, phase)
            vt = k.sb("vt_b", [P, GROUPS * TPB * HG * EB])
            o = k.sb("o_b", [P, GROUPS * TPB * HG * EB])
            prepare(nc, "b", xT, [[wb[:, i, :]] for i in range(4)], (wv[:, :], vt, None, EB), fill, bank,
                    again=True)
            attention(nc, "b", 2, qs, ks, vt, o, bank, ident, identb, EB, lamv[:, 5:6],
                      fill, beside=minus_lambda)

            experts(nc, "f2", x, xT, xn, d, bank, ident, tables, (sorted_x, sorted_y),
                    before=lambda k: ProjectOut(k, "b", o[:, :], EB, [wc[:, 0, :], wc[:, 1, :]], x, xT[:, :], bank,
                                                ident, rms=True),
                    room=Room(qs), out=out)


def feature_order():
    a, dim, pair = np.meshgrid(np.arange(2), np.arange(DH), np.arange(H // 2), indexing="ij")
    return ((2 * pair + a) * DH + dim).reshape(-1)


def constants():
    inv = (1.0 / 10000.0 ** (np.arange(0, DH, 2, dtype=np.float32) / DH)).astype(np.float32)
    pos = (np.arange(P)[None, :] * TPB + np.arange(TPB)[:, None]).reshape(-1).astype(np.float32)
    theta = (pos[None, :] * inv[:, None]).astype(np.float32)
    row = feature_order() % DH // 2
    sign = np.where(feature_order() % 2 == 0, -1.0, 1.0).astype(np.float32)
    return {"cos": np.cos(theta).astype(np.float32)[row],
            "sin": (np.sin(theta).astype(np.float32)[row] * sign[:, None]).astype(np.float32),
            "ident": np.eye(P, dtype=np.float32),
            "earlier": np.triu(np.ones((P, P), np.float32), 1),
            "number": np.arange(24, dtype=np.float32),
            "upto": np.tril(np.ones((E, E), np.float32)).reshape(-1)}


def kernel(**inputs):
    import concourse.bacc as bacc
    from concourse.bass_utils import run_bass_kernel_spmd

    g = {n: np.asarray(v) for n, v in inputs.items()}
    own = feature_order()
    other = own ^ 1
    a, b, f = "L0_attn_a_", "L0_attn_b_", "L0_ffn_"
    arrays = {
        "x": g[a + "x"],
        "WqT": g[a + "Wq"][own].T, "WqT2": g[a + "Wq"][other].T,
        "WkT": g[a + "Wk"][own].T, "WkT2": g[a + "Wk"][other].T,
        "WvT": g[a + "Wv"].T, "WoT": g[a + "Wo"].T,
        "bq": g[a + "bq"][own], "bq2": g[a + "bq"][other], "bk": g[a + "bk"][own], "bk2": g[a + "bk"][other],
        "bv": g[a + "bv"], "bo": g[a + "bo"],
        "q1T": g[b + "q1_w"][own].T, "k1T": g[b + "k1_w"][own].T,
        "q2T": g[b + "q2_w"][own].T, "k2T": g[b + "k2_w"][own].T,
        "vT": g[b + "v_w"].T, "cT": g[b + "c_w"].T,
        "gamma": g[b + "bn_gamma"], "beta": g[b + "bn_beta"], "subln": np.tile(g[b + "subln_w"], P // (2 * DH)),
        "lq1": g[b + "lq1"], "lk1": g[b + "lk1"], "lq2": g[b + "lq2"], "lk2": g[b + "lk2"],
        "gate_w": g[f + "gate_w"], "w1": g[f + "w1"], "b1": g[f + "b1"].reshape(E, FC, P).transpose(2, 0, 1),
        "w2": g[f + "w2"], "b2": g[f + "b2"],
        **constants(),
    }
    nc = bacc.Bacc("TRN2", target_bir_lowering=False, num_devices=1)
    named, d = {}, {}
    for name, v in arrays.items():
        v = np.ascontiguousarray(v)
        named[f"in_{name}"] = v
        d[name] = nc.dram_tensor(f"in_{name}", v.shape, mybir.dt.from_np(v.dtype), kind="ExternalInput").ap()
    out = nc.dram_tensor("out_x", (B, N, D), F32, kind="ExternalOutput").ap()
    hybrid_kernel(nc, d, out)
    r = run_bass_kernel_spmd(nc, [named], core_ids=[0])
    return r.results[0]["out_x"]
```
